# Optimizing a Trainium2 kernel written in Bass

```python
import numpy as np
import jax
import jax.numpy as jnp

def _softmax(x, axis=-1):
    return jax.nn.softmax(x, axis=axis)

def _gelu(x):
    return jax.nn.gelu(x, approximate=True)

def _silu(x):
    return jax.nn.silu(x)

def _sigmoid(x):
    return jax.nn.sigmoid(x)

def _layernorm(x, axis=-1, eps=1e-05):
    m = jnp.mean(x, axis=axis, keepdims=True)
    v = jnp.var(x, axis=axis, keepdims=True)
    return (x - m) / jnp.sqrt(v + eps)

def _scatter_add(tgt, idx, src, axis=0):
    return tgt.at[idx].add(src)

def _segment_sum(src, seg, n):
    return jax.ops.segment_sum(src, seg, n)
kernel_name = 'mk_prb_d1_jaxref_r4_0c0792'

def setup_inputs(seed: int=0):
    np.random.seed(seed)
    _w = jnp.asarray

    def _L0_attn_setup():
        import jax, jax.numpy as jnp
        import numpy as np
        import math
        B, L, D = (2, 512, 256)
        H, KV, HD = (16, 4, 64)
        GROUPS = H // KV
        ROPE_BASE = 10000.0

        def _alibi_slopes(n_heads):

            def pow2(n):
                start = 2.0 ** (-2.0 ** (-(math.log2(n) - 3)))
                return [start * start ** i for i in range(n)]
            if math.log2(n_heads).is_integer():
                return pow2(n_heads)
            c = 2 ** math.floor(math.log2(n_heads))
            return pow2(c) + _alibi_slopes(2 * c)[0::2][:n_heads - c]

        def _rope_cos_sin(seq_len, dim, dtype):
            inv_freq = 1.0 / ROPE_BASE ** (jnp.arange(0, dim, 2, dtype=jnp.float32) / dim)
            t = jnp.arange(seq_len, dtype=jnp.float32)
            freqs = t[:, None] * inv_freq[None, :]
            emb = jnp.concatenate([freqs, freqs], axis=-1)
            return (jnp.cos(emb).astype(dtype), jnp.sin(emb).astype(dtype))

        def _rotate_half(x):
            x1, x2 = (x[..., :x.shape[-1] // 2], x[..., x.shape[-1] // 2:])
            return jnp.concatenate([-x2, x1], axis=-1)
        key = jax.random.key(seed)
        ks = jax.random.split(key, 5)
        s = 0.02
        return {'x': jax.random.normal(ks[0], (B, L, D), jnp.float32), 'Wq': jax.random.normal(ks[1], (D, H * HD), jnp.float32) * s, 'Wk': jax.random.normal(ks[2], (D, KV * HD), jnp.float32) * s, 'Wv': jax.random.normal(ks[3], (D, KV * HD), jnp.float32) * s, 'Wo': jax.random.normal(ks[4], (H * HD, D), jnp.float32) * s}
    _L0_attn_in = _L0_attn_setup()

    def _L0_ffn_setup():
        import jax, jax.numpy as jnp
        import numpy as np
        CAPACITY_FACTOR = 0.5
        key = jax.random.key(seed)
        ks = jax.random.split(key, 5)
        B, S, D, F = (4, 1024, 256, 1024)
        scale_in = 1.0 / np.sqrt(D)
        scale_ff = 1.0 / np.sqrt(F)
        return {'hidden_states': jax.random.normal(ks[0], (B, S, D), dtype=jnp.float32), 'w_router': jax.random.normal(ks[1], (D,), dtype=jnp.float32) * scale_in, 'W1': jax.random.normal(ks[2], (D, F), dtype=jnp.float32) * scale_in, 'b1': jnp.zeros((F,), dtype=jnp.float32), 'W2': jax.random.normal(ks[3], (F, D), dtype=jnp.float32) * scale_ff, 'b2': jnp.zeros((D,), dtype=jnp.float32)}
    _L0_ffn_in = _L0_ffn_setup()
    _d = {'L0_attn_x': _L0_attn_in['x'], 'L0_attn_Wq': _L0_attn_in['Wq'], 'L0_attn_Wk': _L0_attn_in['Wk'], 'L0_attn_Wv': _L0_attn_in['Wv'], 'L0_attn_Wo': _L0_attn_in['Wo'], 'L0_ffn_w_router': _L0_ffn_in['w_router'], 'L0_ffn_W1': _L0_ffn_in['W1'], 'L0_ffn_b1': _L0_ffn_in['b1'], 'L0_ffn_W2': _L0_ffn_in['W2'], 'L0_ffn_b2': _L0_ffn_in['b2']}
    _x0 = _d['L0_attn_x']
    _d['L0_attn_x'] = jax.random.normal(jax.random.fold_in(jax.random.key(seed), 1), (8, 512, 256), dtype=_x0.dtype)
    del _x0
    return _d

def reference(L0_attn_x, L0_attn_Wq, L0_attn_Wk, L0_attn_Wv, L0_attn_Wo, L0_ffn_w_router, L0_ffn_W1, L0_ffn_b1, L0_ffn_W2, L0_ffn_b2):

    def _L0_attn_ref(x, Wq, Wk, Wv, Wo):
        import jax, jax.numpy as jnp
        import numpy as np
        import math
        B, L, D = (2, 512, 256)
        H, KV, HD = (16, 4, 64)
        GROUPS = H // KV
        ROPE_BASE = 10000.0

        def _alibi_slopes(n_heads):

            def pow2(n):
                start = 2.0 ** (-2.0 ** (-(math.log2(n) - 3)))
                return [start * start ** i for i in range(n)]
            if math.log2(n_heads).is_integer():
                return pow2(n_heads)
            c = 2 ** math.floor(math.log2(n_heads))
            return pow2(c) + _alibi_slopes(2 * c)[0::2][:n_heads - c]

        def _rope_cos_sin(seq_len, dim, dtype):
            inv_freq = 1.0 / ROPE_BASE ** (jnp.arange(0, dim, 2, dtype=jnp.float32) / dim)
            t = jnp.arange(seq_len, dtype=jnp.float32)
            freqs = t[:, None] * inv_freq[None, :]
            emb = jnp.concatenate([freqs, freqs], axis=-1)
            return (jnp.cos(emb).astype(dtype), jnp.sin(emb).astype(dtype))

        def _rotate_half(x):
            x1, x2 = (x[..., :x.shape[-1] // 2], x[..., x.shape[-1] // 2:])
            return jnp.concatenate([-x2, x1], axis=-1)
        b, l, _ = x.shape
        q = (x @ Wq).reshape(b, l, H, HD).transpose(0, 2, 1, 3)
        k = (x @ Wk).reshape(b, l, KV, HD).transpose(0, 2, 1, 3)
        v = (x @ Wv).reshape(b, l, KV, HD).transpose(0, 2, 1, 3)
        k = jnp.repeat(k, GROUPS, axis=1)
        v = jnp.repeat(v, GROUPS, axis=1)
        cos, sin = _rope_cos_sin(l, HD, x.dtype)
        q = q * cos + _rotate_half(q) * sin
        k = k * cos + _rotate_half(k) * sin
        attn = jnp.einsum('bhqd,bhkd->bhqk', q, k) / math.sqrt(HD)
        pos = jnp.arange(l)
        rel = (pos[None, :] - pos[:, None]).astype(x.dtype)
        slopes = jnp.asarray(_alibi_slopes(H), dtype=x.dtype)
        attn = attn + slopes[None, :, None, None] * rel[None, None, :, :]
        attn = jax.nn.softmax(attn, axis=-1)
        out = jnp.einsum('bhqk,bhkd->bhqd', attn, v)
        out = out.transpose(0, 2, 1, 3).reshape(b, l, H * HD)
        return out @ Wo

    def _L0_ffn_ref(hidden_states, w_router, W1, b1, W2, b2):
        import jax, jax.numpy as jnp
        import numpy as np
        CAPACITY_FACTOR = 0.5
        'Mixture-of-Depths block: route top-k tokens through an FFN inner block,\n            scatter back with sigmoid router weights; bypassed tokens pass through.'
        B, S, D = hidden_states.shape
        k = int(S * CAPACITY_FACTOR)
        scores = jnp.einsum('bsd,d->bs', hidden_states, w_router)
        top_scores, top_idx = jax.lax.top_k(scores, k)
        weights = jax.nn.sigmoid(top_scores)
        selected = jnp.take_along_axis(hidden_states, top_idx[:, :, None], axis=1)
        h = jax.nn.gelu(jnp.einsum('bkd,df->bkf', selected, W1) + b1)
        processed = jnp.einsum('bkf,fd->bkd', h, W2) + b2
        update = weights[:, :, None] * processed

        def scatter_one(xb, ib, ub):
            return xb.at[ib].add(ub)
        output = jax.vmap(scatter_one)(hidden_states, top_idx, update)
        return output
    x = L0_attn_x
    xn = _layernorm(x, axis=-1)
    x = x + _L0_attn_ref(xn, L0_attn_Wq, L0_attn_Wk, L0_attn_Wv, L0_attn_Wo) + _L0_ffn_ref(xn, L0_ffn_w_router, L0_ffn_W1, L0_ffn_b1, L0_ffn_W2, L0_ffn_b2)
    return x

_drawn_inputs = setup_inputs


def setup_inputs(seed=0):
    import zlib

    import numpy as np

    out = dict(_drawn_inputs(seed))
    spreads = {'L0_ffn_b1': (0.0, 0.505), 'L0_ffn_b2': (0.0, 0.347)}
    factors = {'L0_attn_Wq': 8.0, 'L0_attn_Wk': 8.0}
    for name, (base, spread) in spreads.items():
        noise = np.random.default_rng([zlib.crc32(name.encode()), seed]).standard_normal(out[name].shape)
        drawn = base * np.exp(spread * noise) if base else spread * noise
        out[name] = jnp.asarray(drawn.astype(out[name].dtype))
    for name, factor in factors.items():
        out[name] = (out[name] * factor).astype(out[name].dtype)
    return out
```

```python
import math
from contextlib import ExitStack

import numpy as np
import concourse.bass as bass
import concourse.mybir as mybir

F32 = mybir.dt.float32
F32R = mybir.dt.float32r
BF16 = mybir.dt.bfloat16
ALU = mybir.AluOpType
ACT = mybir.ActivationFunctionType
AX = mybir.AxisListType

P = 128
B, L, D = 8, 512, 256
H, KV, HD = 16, 4, 64
G = H // KV
F = 1024
TT = L // P
DK = D // P
FC = F // P
SEL = L // 2
RT = SEL // P
STEPS = B * KV
EPS = 1e-5
ROW_SLOPE, ROW_MAX, ROWS = HD, HD + 2, HD + 4


def past(b, n):
    return not isinstance(b, int) or b >= n


def phase_one(nc, dram, ctx):
    def sb(name, shape, dt=F32):
        return ctx.enter_context(nc.sbuf_tensor(name, shape, dt))

    def ps(name):
        return ctx.enter_context(nc.psum_tensor(name, [P, 512], F32))

    def sem(name):
        return ctx.enter_context(nc.semaphore(name))

    W1h, W1l = sb("W1h", [P, DK, F], F32R), sb("W1l", [P, DK, F], F32R)
    W2h, W2l = sb("W2h", [P, FC, D], F32R), sb("W2l", [P, FC, D], F32R)
    stage = sb("stage", [P, 2, FC * D])
    ident, iota = sb("ident", [P, P]), sb("iota", [P, SEL])
    iotac, earlier = sb("iotac", [P, RT]), sb("earlier", [P, TT, L])
    router, bias1, bias2 = sb("router", [P, D]), sb("bias1", [P, FC]), sb("bias2", [P, RT, D])
    mhalf = sb("mhalf", [P, TT])
    x, xn, res = (sb(n, [P, 2, TT, D]) for n in ("x", "xn", "res"))
    xh, xl = sb("xh", [P, 2, TT, D], F32R), sb("xl", [P, 2, TT, D], F32R)
    xTh, xTl = sb("xTh", [P, 2, DK, L], F32R), sb("xTl", [P, 2, DK, L], F32R)
    stats, both, mean = sb("stats", [P, 2, TT, 6]), sb("both", [P, 3, TT, 2]), sb("mean", [P, 2, TT])
    vare, rstd = sb("vare", [P, 2, TT]), sb("rstd", [P, 2, TT])
    score, th, wt = sb("score", [P, 2, TT]), sb("th", [P, 2, TT]), sb("wt", [P, 2, TT])
    prod = sb("prod", [P, TT, D], BF16)
    srow, cmp = sb("srow", [P, L]), sb("cmp", [P, 2, L], BF16)
    rk, rank = sb("rk", [P, 2, 2, TT]), sb("rank", [P, 2, TT])
    Gm, GT = sb("Gm", [P, 2, TT, SEL], F32R), sb("GT", [P, 2, RT, L], F32R)
    xsh, xsl = sb("xsh", [P, DK * SEL], F32R), sb("xsl", [P, DK * SEL], F32R)
    g = sb("g", [P, FC, SEL])
    gh, gl = sb("gh", [P, FC, SEL], F32R), sb("gl", [P, FC, SEL], F32R)
    y = sb("y", [P, RT * D])
    yh, yl = sb("yh", [P, RT * D], F32R), sb("yl", [P, RT * D], F32R)
    rs = sb("rs", [P, TT, D])

    bank_xt = [ps("bank_xt0"), ps("bank_xt1")]
    bank_row = ps("bank_row")
    bank_sel = [ps("bank_sel0"), ps("bank_sel1")]
    bank_h = [ps("bank_h0"), ps("bank_h1")]
    bank_y = ps("bank_y")

    w_in, c_in, x_in = sem("w_in"), sem("c_in"), sem("x_in")
    w_hi, w_lo, mh_set = sem("w_hi"), sem("w_lo"), sem("mh_set")
    bn_done, ag_done, vare_done, rstd_done = sem("bn_done"), sem("ag_done"), sem("vare_done"), sem("rstd_done")
    xn_done, xh_done, xl_done, res_done = sem("xn_done"), sem("xh_done"), sem("xl_done"), sem("res_done")
    xt_mm, xth_done, xtl_done, xt_out = sem("xt_mm"), sem("xth_done"), sem("xtl_done"), sem("xt_out")
    score_done, srow_mm, srow_done = sem("score_done"), sem("srow_mm"), sem("srow_done")
    th_done, wt_done = sem("th_done"), sem("wt_done")
    cmp_done, rank_done, rrow_mm = sem("cmp_done"), sem("rank_done"), sem("rrow_mm")
    g_done, gt_done = sem("g_done"), sem("gt_done")
    sel_mm, sel_done, h_mm, gelu_done = sem("sel_mm"), sem("sel_done"), sem("h_mm"), sem("gelu_done")
    gh_done, gl_done, y_mm, y_done = sem("gh_done"), sem("gl_done"), sem("y_mm"), sem("y_done")
    yh_done, yl_done, scat_mm, rs_done, rs_out = (
        sem("yh_done"), sem("yl_done"), sem("scat_mm"), sem("rs_done"), sem("rs_out"))

    def pipeline(eng, step):
        step(0, None, 0)
        step(1, 0, 1)
        with eng.Fori(1, B // 2) as i:
            step(2 * i, 2 * i - 1, 0)
            step(2 * i + 1, 2 * i, 1)
        step(None, B - 1, 0)

    block = ctx.enter_context(nc.Block())

    @block.sync
    def _(sp):
        def load_x(b, par):
            if past(b, 2):
                sp.wait_ge(res_done, b - 1)
            sp.dma_start(x[:, par], dram["x"][b].rearrange("(t p) d -> p t d", p=P)).then_inc(x_in, 16)

        load_x(0, 0)
        sp.dma_start(ident[:], dram["ident"]).then_inc(c_in, 16)
        sp.dma_start(router[:], dram["router"].to_broadcast([P, D])).then_inc(c_in, 16)
        sp.dma_start(iota[:], dram["iota"].to_broadcast([P, SEL])).then_inc(c_in, 16)
        sp.dma_start(iotac[:], dram["iotac"]).then_inc(c_in, 16)
        sp.dma_start(earlier[:], dram["earlier"]).then_inc(c_in, 16)
        sp.dma_start(bias1[:], dram["b1"]).then_inc(c_in, 16)
        for r in range(RT):
            sp.dma_start(bias2[:, r], dram["b2"].to_broadcast([P, D])).then_inc(c_in, 16)
        sp.dma_start(stage[:, 0], dram["W1"]).then_inc(w_in, 16)
        sp.dma_start(stage[:, 1], dram["W2"]).then_inc(w_in, 16)
        load_x(1, 1)

        def step(f, b, par):
            if f is not None:
                sp.wait_ge(xth_done, DK * (f + 1))
                sp.wait_ge(xtl_done, DK * (f + 1))
                sp.dma_start(dram["xt"][f, 0].bitcast(F32), xTh[:, par].bitcast(F32)).then_inc(xt_out, 16)
                sp.dma_start(dram["xt"][f, 1].bitcast(F32), xTl[:, par].bitcast(F32)).then_inc(xt_out, 16)
            if b is not None:
                if not isinstance(b, int) or b + 2 < B:
                    load_x_next(b, 1 - par)
                sp.wait_ge(rs_done, TT * (b + 1))
                sp.dma_start(dram["res"][b].rearrange("(t p) d -> p t d", p=P), rs[:]).then_inc(rs_out, 16)

        def load_x_next(b, par):
            load_x(b + 2, par)

        step(0, None, 0)
        step(1, 0, 1)
        with sp.Fori(1, B // 2 - 1) as i:
            step(2 * i, 2 * i - 1, 0)
            step(2 * i + 1, 2 * i, 1)
        step(B - 2, B - 3, 0)
        step(B - 1, B - 2, 1)
        step(None, B - 1, 0)
        sp.wait_ge(rs_out, 16 * B)
        sp.wait_ge(xt_out, 2 * 16 * B)

    @block.gpsimd
    def _(pool):
        pool.memset(mhalf[:], -0.5).then_inc(mh_set, 1)

        def step(f, b, par):
            if f is None:
                return
            if isinstance(f, int) and f == 0:
                pool.wait_ge(mh_set, 1)
            pool.wait_ge(vare_done, f + 1)
            pool.tensor_tensor(rstd[:, par], vare[:, par], mhalf[:], ALU.pow).then_inc(rstd_done, 1)
            pool.wait_ge(xn_done, TT * (f + 1))
            if past(f, 2):
                pool.wait_ge(rs_done, TT * (f - 1))
            pool.tensor_tensor(res[:, par], x[:, par], xn[:, par], ALU.add).then_inc(res_done, 1)
            pool.wait_ge(xh_done, f + 1)
            if past(f, 2):
                pool.wait_ge(sel_mm, 2 * (f - 1))
            pool.tensor_tensor(xl[:, par], xn[:, par], xh[:, par].bitcast(F32), ALU.subtract).then_inc(xl_done, 1)

        pipeline(pool, step)

    @block.scalar
    def _(act):
        act.wait_ge(w_in, 32)
        act.activation(W1h[:].rearrange("p k n -> p (k n)"), stage[:, 0], ACT.Copy).then_inc(w_hi, 1)
        act.activation(W2h[:].rearrange("p k n -> p (k n)"), stage[:, 1], ACT.Copy).then_inc(w_hi, 1)
        act.wait_ge(c_in, 16 * 8)

        def step(f, b, par):
            if b is not None:
                for part, dst in enumerate((xsh, xsl)):
                    act.wait_ge(sel_mm, 2 * b + part + 1)
                    if past(b, 1):
                        act.wait_ge(h_mm, FC // 2 * b)
                    act.activation(dst[:], bank_sel[part][:], ACT.Copy).then_inc(sel_done, 1)
            if f is not None:
                act.wait_ge(xn_done, TT * (f + 1))
                if past(f, 2):
                    act.wait_ge(sel_mm, 2 * (f - 1))
                act.activation(xh[:, par], xn[:, par], ACT.Copy).then_inc(xh_done, 1)
                for k in range(DK):
                    act.wait_ge(xt_mm, DK * f + k + 1)
                    if past(f, 2):
                        act.wait_ge(xt_out, 32 * (f - 1))
                    act.activation(xTh[:, par, k], bank_xt[k][:], ACT.Copy).then_inc(xth_done, 1)
            if b is not None:
                for c2 in range(FC // 2 + 1):
                    if c2 < FC // 2:
                        act.wait_ge(h_mm, FC // 2 * b + c2 + 1)
                        if past(b, 1):
                            act.wait_ge(gl_done, FC // 2 * (b - 1) + c2 + 1)
                        for c in (2 * c2, 2 * c2 + 1):
                            act.activation(g[:, c], bank_h[c2 % 2][:, (c % 2) * SEL:(c % 2 + 1) * SEL],
                                           ACT.Gelu_apprx_tanh, bias=bias1[:, c:c + 1]).then_inc(gelu_done, 1)
                    if c2 > 0:
                        act.wait_ge(gelu_done, FC * b + 2 * c2)
                        if past(b, 1):
                            act.wait_ge(y_mm, RT * b)
                        act.activation(gh[:, 2 * c2 - 2:2 * c2], g[:, 2 * c2 - 2:2 * c2], ACT.Copy).then_inc(gh_done, 1)
            if f is not None:
                act.wait_ge(srow_mm, f + 1)
                if past(f, 1):
                    act.wait_ge(cmp_done, 2 * TT * f)
                act.activation(srow[:], bank_row[:], ACT.Copy).then_inc(srow_done, 1)
                act.wait_ge(score_done, TT * (f + 1))
                if past(f, 2):
                    act.wait_ge(wt_done, f - 1)
                act.activation(th[:, par], score[:, par], ACT.Tanh, scale=0.5).then_inc(th_done, 1)
            if b is not None:
                act.wait_ge(y_done, b + 1)
                if past(b, 1):
                    act.wait_ge(scat_mm, TT * b)
                act.activation(yh[:], y[:], ACT.Copy).then_inc(yh_done, 1)

        pipeline(act, step)

    @block.vector
    def _(dve):
        dve.wait_ge(w_hi, 2)
        dve.tensor_tensor(W1l[:].rearrange("p k n -> p (k n)"), stage[:, 0],
                          W1h[:].rearrange("p k n -> p (k n)").bitcast(F32), ALU.subtract).then_inc(w_lo, 1)
        dve.tensor_tensor(W2l[:].rearrange("p k n -> p (k n)"), stage[:, 1],
                          W2h[:].rearrange("p k n -> p (k n)").bitcast(F32), ALU.subtract).then_inc(w_lo, 1)
        dve.wait_ge(c_in, 16 * 8)

        def step(f, b, par):
            if f is not None:
                dve.wait_ge(x_in, 16 * (f + 1))
                for t in range(TT):
                    dve.bn_stats(stats[:, par, t], x[:, par, t]).then_inc(bn_done, 1)
                dve.wait_ge(bn_done, TT * (f + 1))
                even, odd = stats[:, par, :, 1:3], stats[:, par, :, 4:6]
                dve.tensor_tensor(both[:, 0], even, odd, ALU.add).then_inc(ag_done, 1)
                dve.tensor_tensor(both[:, 1], even, odd, ALU.subtract).then_inc(ag_done, 1)
                dve.wait_ge(ag_done, 5 * f + 2)
                dve.tensor_scalar(mean[:, par], both[:, 0, :, 0], 0.5, None, ALU.mult).then_inc(ag_done, 1)
                dve.tensor_scalar(both[:, 2, :, 0], both[:, 0, :, 1], 1.0 / D, EPS, ALU.mult, ALU.add).then_inc(ag_done, 1)
                dve.scalar_tensor_tensor(out=both[:, 2, :, 1], in0=both[:, 1, :, 0], scalar=0.25, in1=both[:, 1, :, 0],
                                         op0=ALU.mult, op1=ALU.mult).then_inc(ag_done, 1)
                dve.wait_ge(ag_done, 5 * (f + 1))
                dve.tensor_tensor(vare[:, par], both[:, 2, :, 0], both[:, 2, :, 1], ALU.add).then_inc(vare_done, 1)
                dve.wait_ge(rstd_done, f + 1)
                if past(f, 2):
                    dve.wait_ge(xl_done, f - 1)
                    dve.wait_ge(xt_mm, DK * (f - 1))
                    dve.wait_ge(score_done, TT * (f - 1))
                for t in range(TT):
                    dve.tensor_scalar(xn[:, par, t], x[:, par, t], mean[:, par, t:t + 1], rstd[:, par, t:t + 1],
                                      ALU.subtract, ALU.mult).then_inc(xn_done, 1)
                dve.wait_ge(xn_done, TT * (f + 1))
                for t in range(TT):
                    dve.tensor_tensor_reduce(out=prod[:, t], in0=xn[:, par, t], in1=router[:], scale=1.0, scalar=0.0,
                                             op0=ALU.mult, op1=ALU.add,
                                             accum_out=score[:, par, t:t + 1]).then_inc(score_done, 1)
                for k in range(DK):
                    dve.wait_ge(xth_done, DK * f + k + 1)
                    dve.tensor_tensor(xTl[:, par, k], bank_xt[k][:], xTh[:, par, k].bitcast(F32),
                                      ALU.subtract).then_inc(xtl_done, 1)
            if b is not None:
                for c2 in range(FC // 2):
                    dve.wait_ge(gh_done, FC // 2 * b + c2 + 1)
                    dve.tensor_tensor(gl[:, 2 * c2:2 * c2 + 2], g[:, 2 * c2:2 * c2 + 2],
                                      gh[:, 2 * c2:2 * c2 + 2].bitcast(F32), ALU.subtract).then_inc(gl_done, 1)
            if f is not None:
                dve.wait_ge(srow_done, f + 1)
                for t in range(TT):
                    for part in range(2):
                        n = 2 * TT * f + 2 * t + part
                        if past(n, 2):
                            dve.wait_ge(cmp_done, n - 1)
                        own = score[:, par, t:t + 1]
                        if part == 0:
                            dve.tensor_scalar(cmp[:, part], srow[:], own, None, ALU.is_gt, ALU.add,
                                              accum_out=rk[:, par, 0, t:t + 1]).then_inc(cmp_done, 1)
                        else:
                            dve.scalar_tensor_tensor(out=cmp[:, part], in0=srow[:], scalar=own, in1=earlier[:, t],
                                                     op0=ALU.is_equal, op1=ALU.mult,
                                                     accum_out=rk[:, par, 1, t:t + 1]).then_inc(cmp_done, 1)
                dve.wait_ge(cmp_done, 2 * TT * (f + 1))
                if past(f, 2):
                    dve.wait_ge(rrow_mm, f - 1)
                dve.tensor_tensor(rank[:, par], rk[:, par, 0], rk[:, par, 1], ALU.add).then_inc(rank_done, 1)
                dve.wait_ge(th_done, f + 1)
                if past(f, 2):
                    dve.wait_ge(rs_done, TT * (f - 1))
                dve.tensor_scalar(wt[:, par], th[:, par], 0.5, 0.5, ALU.mult, ALU.add).then_inc(wt_done, 1)
            if b is not None:
                dve.wait_ge(y_mm, RT * (b + 1))
                if past(b, 1):
                    dve.wait_ge(yl_done, b)
                dve.tensor_tensor(y[:], bank_y[:], bias2[:].rearrange("p r n -> p (r n)"), ALU.add).then_inc(y_done, 1)
            if f is not None:
                dve.wait_ge(rank_done, f + 1)
                if past(f, 2):
                    dve.wait_ge(sel_mm, 2 * (f - 1))
                for t in range(TT):
                    dve.tensor_scalar(Gm[:, par, t], iota[:], rank[:, par, t:t + 1], None,
                                      ALU.is_equal).then_inc(g_done, 1)
            if b is not None:
                dve.wait_ge(yh_done, b + 1)
                dve.tensor_tensor(yl[:], y[:], yh[:].bitcast(F32), ALU.subtract).then_inc(yl_done, 1)
            if f is not None:
                dve.wait_ge(rrow_mm, f + 1)
                if past(f, 2):
                    dve.wait_ge(scat_mm, TT * (f - 1))
                for r in range(RT):
                    dve.tensor_scalar(GT[:, par, r], bank_row[:], iotac[:, r:r + 1], None,
                                      ALU.is_equal).then_inc(gt_done, 1)
            if b is not None:
                back = 1 - par
                dve.wait_ge(res_done, b + 1)
                dve.wait_ge(wt_done, b + 1)
                if past(b, 1):
                    dve.wait_ge(rs_out, 16 * b)
                for t in range(TT):
                    dve.wait_ge(scat_mm, TT * b + 2 * (t // 2) + 2)
                    dve.scalar_tensor_tensor(out=rs[:, t], in0=bank_sel[t // 2][:, (t % 2) * D:(t % 2 + 1) * D],
                                             scalar=wt[:, back, t:t + 1], in1=res[:, back, t],
                                             op0=ALU.mult, op1=ALU.add).then_inc(rs_done, 1)

        pipeline(dve, step)

    @block.tensor
    def _(pe):
        pe.wait_ge(c_in, 16 * 8)
        pe.wait_ge(w_lo, 2)

        def step(f, b, par):
            back = 1 - par
            if b is not None:
                pe.wait_ge(g_done, TT * (b + 1))
                pe.wait_ge(xl_done, b + 1)
                if past(b, 1):
                    pe.wait_ge(rs_done, TT * b)
                for part, src in enumerate((xh, xl)):
                    for k in range(DK):
                        for t in range(TT):
                            last = pe.matmul(bank_sel[part][:, k * SEL:(k + 1) * SEL],
                                             src[:, back, t, k * P:(k + 1) * P], Gm[:, back, t],
                                             start=(t == 0), stop=(t == TT - 1))
                    last.then_inc(sel_mm, 1)
            if f is not None:
                pe.wait_ge(xn_done, TT * (f + 1))
                if past(f, 1):
                    pe.wait_ge(xtl_done, DK * f)
                for k in range(DK):
                    for t in range(TT):
                        last = pe.transpose(bank_xt[k][:, t * P:(t + 1) * P], xn[:, par, t, k * P:(k + 1) * P], ident[:])
                    last.then_inc(xt_mm, 1)
            if b is not None:
                pe.wait_ge(sel_done, 2 * (b + 1))
                for c2 in range(FC // 2):
                    if past(b, 1) or c2 >= 2:
                        pe.wait_ge(gelu_done, FC * b + 2 * (c2 - 1))
                    for c in (2 * c2, 2 * c2 + 1):
                        out = bank_h[c2 % 2][:, (c % 2) * SEL:(c % 2 + 1) * SEL]
                        n = 0
                        for w, xs in ((W1h, xsh), (W1l, xsh), (W1h, xsl)):
                            for k in range(DK):
                                last = pe.matmul(out, w[:, k, c * P:(c + 1) * P], xs[:, k * SEL:(k + 1) * SEL],
                                                 start=(n == 0), stop=(n == 3 * DK - 1))
                                n += 1
                    last.then_inc(h_mm, 1)
            if f is not None:
                pe.wait_ge(score_done, TT * (f + 1))
                if past(f, 1):
                    pe.wait_ge(gt_done, RT * f)
                for t in range(TT):
                    last = pe.transpose(bank_row[:, t * P:(t + 1) * P],
                                        score[:, par, t:t + 1].to_broadcast([P, P]), ident[:])
                last.then_inc(srow_mm, 1)
            if b is not None:
                if past(b, 1):
                    pe.wait_ge(y_done, b)
                for r in range(RT):
                    n = 0
                    for c in range(FC):
                        if r == 0 and c % 2 == 0:
                            pe.wait_ge(gl_done, FC // 2 * b + c // 2 + 1)
                        for gs, w in ((gh, W2h), (gl, W2h), (gh, W2l)):
                            last = pe.matmul(bank_y[:, r * D:(r + 1) * D], gs[:, c, r * P:(r + 1) * P], w[:, c],
                                             start=(n == 0), stop=(n == 3 * FC - 1))
                            n += 1
                    last.then_inc(y_mm, 1)
            if f is not None:
                pe.wait_ge(rank_done, f + 1)
                pe.wait_ge(srow_done, f + 1)
                for t in range(TT):
                    last = pe.transpose(bank_row[:, t * P:(t + 1) * P],
                                        rank[:, par, t:t + 1].to_broadcast([P, P]), ident[:])
                last.then_inc(rrow_mm, 1)
            if b is not None:
                pe.wait_ge(yl_done, b + 1)
                pe.wait_ge(gt_done, RT * (b + 1))
                for t in range(TT):
                    n = 0
                    for r in range(RT):
                        for part in (yh, yl):
                            last = pe.matmul(bank_sel[t // 2][:, (t % 2) * D:(t % 2 + 1) * D],
                                             GT[:, back, r, t * P:(t + 1) * P], part[:, r * D:(r + 1) * D],
                                             start=(n == 0), stop=(n == 2 * RT - 1))
                            n += 1
                    last.then_inc(scat_mm, 1)

        pipeline(pe, step)


def phase_two(nc, dram, ctx):
    def sb(name, shape, dt=F32):
        return ctx.enter_context(nc.sbuf_tensor("a_" + name, shape, dt))

    def ps(name, shape):
        return ctx.enter_context(nc.psum_tensor("a_" + name, shape, F32))

    def sem(name):
        return ctx.enter_context(nc.semaphore("a_" + name))

    PAIRS = H // 2
    OT = PAIRS // 2
    UNITS = TT * G // 2
    Wqh, Wql = sb("Wqh", [P, DK, KV, 2, P], F32R), sb("Wql", [P, DK, KV, 2, P], F32R)
    Wkh, Wkl = sb("Wkh", [P, DK, 2, P], F32R), sb("Wkl", [P, DK, 2, P], F32R)
    Wvh, Wvl = sb("Wvh", [P, DK, KV * HD], F32R), sb("Wvl", [P, DK, KV * HD], F32R)
    Woh, Wol = sb("Woh", [P, PAIRS, D], F32R), sb("Wol", [P, PAIRS, D], F32R)
    cos, sin = sb("cos", [P, L]), sb("sin", [P, L])
    ident, ones = sb("ident", [P, P]), sb("ones", [P, HD])
    slopes, keyrows = sb("slopes", [P, H]), sb("keyrows", [P, L])
    xT = sb("xT", [P, 2, DK, L], F32R)
    rot = sb("rot", [P, 4, L])
    qs, ks = sb("qs", [P, 4, L], F32R), sb("ks", [P, 4, L], F32R)
    q1, q2 = sb("q1", [P, KV, G, L], F32R), sb("q2", [P, 2, G, L], F32R)
    k1, k2 = sb("k1", [P, KV, L], F32R), sb("k2", [P, KV, L], F32R)
    vs, v = sb("vs", [P, TT, KV * HD]), sb("v", [P, KV, TT, HD])
    mx = sb("mx", [P, 2, P])
    nmh, nml = sb("nmh", [P, P], F32R), sb("nml", [P, P], F32R)
    p = sb("p", [P, TT, 2, L])
    psum = sb("psum", [P, 2, L])
    rden, o_raw, o = sb("rden", [P, L]), sb("o_raw", [P, L]), sb("o", [P, L])
    oh, ol = sb("oh", [P, OT, L], F32R), sb("ol", [P, OT, L], F32R)
    acc = sb("acc", [P, TT, D])

    bank_m, bank_s = ps("bank_m", [P, 2, L]), ps("bank_s", [P, 2, L])
    bank_o, bank_d = ps("bank_o", [P, L]), ps("bank_d", [P, L])
    bank_f = [ps("bank_f0", [P, L]), ps("bank_f1", [P, L])]

    w_in, w_hi, w_lo, c_in = sem("w_in"), sem("w_hi"), sem("w_lo"), sem("c_in")
    rows_set, mem_set = sem("rows_set"), sem("mem_set")
    xt_in, acc_in = sem("xt_in"), sem("acc_in")
    rope_mm, v_mm, wo_mm = sem("rope_mm"), sem("v_mm"), sem("wo_mm")
    rot_mul, rot_sum, rope_hi, rope_lo, v_done = (
        sem("rot_mul"), sem("rot_sum"), sem("rope_hi"), sem("rope_lo"), sem("v_done"))
    q1_in, k_in, v_in = ([sem(f"{n}{g}") for g in range(KV)] for n in ("q1_in", "k_in", "v_in"))
    q2_in, max_in = [sem(f"q2_in{n}") for n in range(2)], sem("max_in")
    max_mm, max_done, maxT_mm, neg_hi, neg_lo = (
        sem("max_mm"), sem("max_done"), sem("maxT_mm"), sem("neg_hi"), sem("neg_lo"))
    score_mm, exp_done, pv_mm, psum_done, den_mm = (
        sem("score_mm"), sem("exp_done"), sem("pv_mm"), sem("psum_done"), sem("den_mm"))
    raw_done = sem("raw_done")
    rden_done, o_done, oh_done, ol_done = sem("rden_done"), sem("o_done"), sem("oh_done"), sem("ol_done")
    acc_done, out_done = sem("acc_done"), sem("out_done")

    Q1_IN, Q2_IN, K_IN, V_IN, MAX_IN = 16 * 2 * G, 16 * 4 * G, 16 * 6, 16, 16 * 2

    ROT_K, ROT_Q = 2, (0, 1, 3, 4)

    def rotation(b, n):
        return 3 + 5 * b + n

    def rotation_of_next_step(b, g):
        return rotation(b, ROT_Q[g - 1]) if g else rotation(b, 0) - 1

    def is_last(b):
        return isinstance(b, int) and b == B - 1

    def batches(eng, body):
        body(0)
        with eng.Fori(1, B - 1) as b:
            body(b)
        body(B - 1)

    def max_unit(b, g, u):
        ahead = g + (1 if u < UNITS // 2 else 2)
        if is_last(b) and ahead >= KV:
            return None
        return b + ahead // KV, ahead % KV, (u + UNITS // 2) % UNITS

    def work(n, size):
        return p[:].rearrange("p t h l -> p (t h l)")[:, n:n + size]

    KVW = DK * KV * HD
    QW = DK * H * HD

    block = ctx.enter_context(nc.Block())

    @block.sync
    def _(sp):
        def load_xt(b):
            sp.dma_start(xT[:].rearrange("p a k l -> p a (k l)").bitcast(F32),
                         dram["xt"][b].rearrange("a p k l -> p a (k l)").bitcast(F32)).then_inc(xt_in, 16)

        def load_acc(b):
            sp.dma_start(acc[:], dram["res"][b].rearrange("(t p) d -> p t d", p=P)).then_inc(acc_in, 16)

        def store_out(b):
            sp.wait_ge(acc_done, 2 * TT * (b + 1))
            sp.dma_start(dram["out"][b].rearrange("(t p) d -> p t d", p=P), acc[:]).then_inc(out_done, 16)

        def place_q1(f, g, r):
            sp.wait_ge(rope_hi, 2 * (r + 1))
            if past(f, 4):
                sp.wait_ge(score_mm, UNITS * (f - 3))
            for h in range(G):
                for half in range(2):
                    sp.dma_start(q1[32 * half:32 * half + 32, g, h].bitcast(F32),
                                 qs[32 * h:32 * h + 32, half].bitcast(F32)).then_inc(q1_in[g], 16)

        def place_k(f, g, r):
            sp.wait_ge(rope_lo, 2 * (r + 1))
            if past(f, 4):
                sp.wait_ge(score_mm, UNITS * (f - 3))
            for half in range(2):
                rows = slice(32 * g, 32 * g + 32)
                at = 32 * half
                for dst, src in ((k1[at:at + 32, g], ks[rows, half]), (k2[HD + at:HD + at + 32, g], ks[rows, half]),
                                 (k2[at:at + 32, g], ks[rows, 2 + half])):
                    sp.dma_start(dst.bitcast(F32), src.bitcast(F32)).then_inc(k_in[g], 16)

        def place_v(f, b, g):
            sp.wait_ge(v_done, 2 * (b + 1))
            if past(f, 4):
                sp.wait_ge(pv_mm, UNITS * (f - 3))
            sp.dma_start(v[:, g], vs[:, :, g * HD:(g + 1) * HD]).then_inc(v_in[g], 16)

        def place_q2(f, slot, r):
            if past(f, 2):
                sp.wait_ge(score_mm, UNITS * (f - 1))
            sp.wait_ge(rope_lo, 2 * (r + 1))
            for h in range(G):
                for n in range(4):
                    sp.dma_start(q2[32 * n:32 * n + 32, slot, h].bitcast(F32),
                                 qs[32 * h:32 * h + 32, n].bitcast(F32)).then_inc(q2_in[slot], 16)

        def place_max(f, g):
            for row, src, ready in ((ROW_MAX, nmh, neg_hi), (ROW_MAX + 1, nml, neg_lo)):
                sp.wait_ge(ready, f + 1)
                sp.dma_start(q1[row:row + 1, g].rearrange("o h (t c) -> o (h t) c", c=P).bitcast(F32),
                             src[0:G * TT, :].bitcast(F32)).then_inc(max_in, 16)

        load_xt(0)
        sp.dma_start(work(0, KVW), dram["Wk"]).then_inc(w_in, 16)
        sp.dma_start(work(QW, QW), dram["Wq"]).then_inc(w_in, 16)
        sp.dma_start(work(KVW, KVW), dram["Wv"]).then_inc(w_in, 16)
        sp.dma_start(cos[:], dram["cos"]).then_inc(c_in, 16)
        sp.dma_start(sin[:], dram["sin"]).then_inc(c_in, 16)
        sp.dma_start(ident[:], dram["ident"]).then_inc(c_in, 16)
        sp.dma_start(slopes[ROW_SLOPE:ROW_MAX, :], dram["slope_rows"]).then_inc(c_in, 16)
        sp.dma_start(keyrows[ROW_SLOPE:ROWS, :], dram["key_rows"]).then_inc(c_in, 16)
        sp.wait_ge(w_lo, 3)
        sp.dma_start(work(0, QW), dram["Wo"]).then_inc(w_in, 16)
        load_acc(0)
        place_q1(0, 0, 1)
        place_q2(0, 0, 1)
        place_k(0, 0, 0)
        place_q1(1, 1, 2)
        place_k(1, 1, 0)
        place_v(0, 0, 0)
        place_v(1, 0, 1)
        place_max(0, 0)

        def body(b):
            for g in range(KV):
                s = 4 * b + g
                if not (is_last(b) and g == KV - 1):
                    place_q2(s + 1, (g + 1) % 2, rotation_of_next_step(b, g))
                if g == 1 and past(b, 1):
                    store_out(b - 1)
                    sp.wait_ge(out_done, 16 * b)
                    load_acc(b)
                if g == 1 and not is_last(b):
                    sp.wait_ge(rope_mm, 2 * rotation(b, ROT_K))
                    load_xt(b + 1)
                if not (is_last(b) and g >= 2):
                    place_q1(s + 2, (g + 2) % KV, rotation(b, ROT_Q[g]))
                    if g < 2:
                        place_k(s + 2, g + 2, key_rotation(b))
                        place_v(s + 2, b, g + 2)
                    else:
                        place_k(s + 2, g - 2, rotation(b, ROT_K))
                        place_v(s + 2, b + 1, g - 2)
                if not (is_last(b) and g == KV - 1):
                    place_max(s + 1, (g + 1) % KV)

        def key_rotation(b):
            return 0 if isinstance(b, int) and b == 0 else rotation(b, ROT_K) - 5

        batches(sp, body)
        store_out(B - 1)
        sp.wait_ge(out_done, 16 * B)

    @block.gpsimd
    def _(pool):
        pool.memset(mx[:], 0.0).then_inc(mem_set, 1)
        pool.memset(ones[:], 1.0).then_inc(mem_set, 1)

        def rotate(r):
            pool.wait_ge(rot_mul, 4 * r + 3)
            pool.tensor_tensor(rot[:, 0], rot[:, 0], rot[:, 1], ALU.subtract).then_inc(rot_sum, 1)
            pool.wait_ge(rot_mul, 4 * r + 4)
            pool.tensor_tensor(rot[:, 2], rot[:, 2], rot[:, 3], ALU.add).then_inc(rot_sum, 1)

        def rotate_lo(r, dst):
            for half in range(2):
                pool.wait_ge(rope_hi, 2 * r + half + 1)
                pool.tensor_tensor(dst[:, 2 + half], rot[:, 2 * half], dst[:, half].bitcast(F32),
                                   ALU.subtract).then_inc(rope_lo, 1)

        def output_lo(r, slot):
            pool.wait_ge(oh_done, r + 1)
            pool.tensor_tensor(ol[:, slot], o[:], oh[:, slot].bitcast(F32), ALU.subtract).then_inc(ol_done, 1)

        for r, dst in ((0, ks), (1, qs), (2, qs)):
            rotate(r)
            rotate_lo(r, dst)

        def body(b):
            for g in range(KV):
                s = 4 * b + g
                queries = not (is_last(b) and g >= 2)
                for u in range(UNITS):
                    n, kt, r = UNITS * s + u, u % TT, 2 * s + u // TT
                    if kt == 1:
                        pool.wait_ge(exp_done, n + 1)
                        if past(b, 1) or r > 0:
                            pool.wait_ge(den_mm, r)
                        pool.tensor_tensor(psum[:], p[:, 0], p[:, 1], ALU.add).then_inc(psum_done, 1)
                    elif kt > 1:
                        pool.wait_ge(exp_done, n + 1)
                        pool.wait_ge(psum_done, 3 * r + kt - 1)
                        pool.tensor_tensor(psum[:], psum[:], p[:, kt], ALU.add).then_inc(psum_done, 1)
                    if u == 0 and g == 2 and not is_last(b):
                        rotate_lo(rotation(b, ROT_K), ks)
                    if u == 2 and queries:
                        rotate(rotation(b, ROT_Q[g]))
                    if u == 4 and queries:
                        rotate_lo(rotation(b, ROT_Q[g]), qs)
                    if u == 4 and (past(b, 1) or g > 0):
                        output_lo(2 * s - 1, (2 * g - 1) % OT)
                    if u == UNITS - 1:
                        if g == 1 and not is_last(b):
                            rotate(rotation(b, ROT_K))
                        output_lo(2 * s, (2 * g) % OT)

        batches(pool, body)
        output_lo(2 * STEPS - 1, OT - 1)

    @block.scalar
    def _(act):
        def copy_hi(dst, src, scale=1.0):
            act.activation(dst, src, ACT.Copy, scale=scale).then_inc(w_hi, 1)

        act.wait_ge(w_in, 3 * 16)
        copy_hi(Wkh[:].rearrange("p k n c -> p (k n c)"), work(0, KVW))
        copy_hi(Wvh[:].rearrange("p k c -> p (k c)"), work(KVW, KVW))
        copy_hi(Wqh[:].rearrange("p k g n c -> p (k g n c)"), work(QW, QW), HD ** -0.5)
        act.wait_ge(c_in, 5 * 16)
        for g in range(KV):
            act.activation(k1[ROW_SLOPE:ROWS, g], keyrows[ROW_SLOPE:ROWS, :], ACT.Copy).then_inc(rows_set, 1)
        for g in range(KV):
            act.activation(q1[ROW_SLOPE:ROW_MAX, g],
                           slopes[ROW_SLOPE:ROW_MAX, g * G:(g + 1) * G].rearrange("p (h o) -> p h o", o=1)
                           .to_broadcast([ROW_MAX - ROW_SLOPE, G, L]), ACT.Copy).then_inc(rows_set, 1)
        def rotate_hi(r, dst):
            for half in range(2):
                act.wait_ge(rot_sum, 2 * r + half + 1)
                act.activation(dst[:, half], rot[:, 2 * half], ACT.Copy).then_inc(rope_hi, 1)

        def queries_hi(r, b, g):
            if past(b, 1) or g > 0:
                placed, last = (b, g - 1) if g else (b - 1, KV - 1)
                act.wait_ge(q1_in[last], Q1_IN * (placed + 1))
                act.wait_ge(q2_in[last % 2], Q2_IN * (2 * placed + last // 2 + 1))
            rotate_hi(r, qs)

        def values(b):
            for half in range(2):
                act.wait_ge(v_mm, 2 * b + half + 1)
                if past(b, 1):
                    for g in range(KV):
                        act.wait_ge(v_in[g], V_IN * b)
                act.activation(vs[:, 2 * half:2 * half + 2].rearrange("p t d -> p (t d)"), bank_f[half][:],
                               ACT.Copy).then_inc(v_done, 1)

        def output_raw(r):
            act.wait_ge(pv_mm, TT * (r + 1))
            if past(r, 1):
                act.wait_ge(o_done, r)
            act.activation(o_raw[:], bank_o[:], ACT.Copy).then_inc(raw_done, 1)

        def output_hi(r, slot, b, g):
            act.wait_ge(o_done, r + 1)
            if g >= 2:
                act.wait_ge(wo_mm, 2 * TT * b + TT)
            elif past(b, 1):
                act.wait_ge(wo_mm, 2 * TT * b)
            act.activation(oh[:, slot], o[:], ACT.Copy).then_inc(oh_done, 1)

        rotate_hi(0, ks)
        queries_hi(1, 0, 0)
        queries_hi(2, 0, 1)
        values(0)
        act.wait_ge(w_in, 4 * 16)
        copy_hi(Woh[:].rearrange("p k c -> p (k c)"), work(0, QW))

        def body(b):
            for g in range(KV):
                s = 4 * b + g
                queries = not (is_last(b) and g >= 2)
                for u in range(UNITS):
                    n, kt, r = UNITS * s + u, u % TT, 2 * s + u // TT
                    act.wait_ge(score_mm, n + 1)
                    if past(b, 1) or n >= TT:
                        act.wait_ge(pv_mm, n - TT + 1)
                        act.wait_ge(psum_done, 3 * (r - 1) + max(kt, 1))
                    if isinstance(b, int) and b == 0 and n < 1:
                        act.wait_ge(w_lo, 4)
                    act.activation(p[:, kt], bank_s[:], ACT.Exp).then_inc(exp_done, 1)
                    if u == 0 and g == 2 and not is_last(b):
                        for slot in range(KV):
                            act.wait_ge(k_in[slot], K_IN * (b + 1))
                        rotate_hi(rotation(b, ROT_K), ks)
                    if u == 0 and (past(b, 1) or g > 0):
                        output_raw(2 * s - 1)
                    if u == 4:
                        output_raw(2 * s)
                    if u == 3 and queries:
                        queries_hi(rotation(b, ROT_Q[g]), b + (g + 2) // KV, (g + 2) % KV)
                    if u == 4 and (past(b, 1) or g > 0):
                        output_hi(2 * s - 1, (2 * g - 1) % OT, *((b, g - 1) if g else (b - 1, KV - 1)))
                    if u == 4 and g == 2 and not is_last(b):
                        values(b + 1)
                    if u == UNITS - 1:
                        output_hi(2 * s, (2 * g) % OT, b, g)

        batches(act, body)
        output_raw(2 * STEPS - 1)
        output_hi(2 * STEPS - 1, OT - 1, B - 1, KV - 1)

    @block.vector
    def _(dve):
        def lo(dst, src, hi, scale=1.0):
            dve.scalar_tensor_tensor(out=dst, in0=src, scalar=scale, in1=hi, op0=ALU.mult,
                                     op1=ALU.subtract).then_inc(w_lo, 1)

        dve.wait_ge(w_hi, 1)
        lo(Wkl[:].rearrange("p k n c -> p (k n c)"), work(0, KVW), Wkh[:].rearrange("p k n c -> p (k n c)").bitcast(F32))
        dve.wait_ge(w_hi, 2)
        lo(Wvl[:].rearrange("p k c -> p (k c)"), work(KVW, KVW), Wvh[:].rearrange("p k c -> p (k c)").bitcast(F32))
        dve.wait_ge(w_hi, 3)
        lo(Wql[:].rearrange("p k g n c -> p (k g n c)"), work(QW, QW),
           Wqh[:].rearrange("p k g n c -> p (k g n c)").bitcast(F32), HD ** -0.5)
        dve.wait_ge(c_in, 5 * 16)
        dve.wait_ge(mem_set, 1)

        def rotate(r):
            dve.wait_ge(rope_mm, 2 * r + 1)
            if past(r, 1):
                dve.wait_ge(rope_hi, 2 * r)
                dve.wait_ge(rope_lo, 2 * r)
            dve.tensor_tensor(rot[:, 0], bank_f[0][:], cos[:], ALU.mult).then_inc(rot_mul, 1)
            dve.tensor_tensor(rot[:, 3], bank_f[0][:], sin[:], ALU.mult).then_inc(rot_mul, 1)
            dve.wait_ge(rope_mm, 2 * r + 2)
            dve.tensor_tensor(rot[:, 1], bank_f[1][:], sin[:], ALU.mult).then_inc(rot_mul, 1)
            dve.tensor_tensor(rot[:, 2], bank_f[1][:], cos[:], ALU.mult).then_inc(rot_mul, 1)

        def maxima(b, g, i):
            f, parity = 4 * b + g, g % 2
            dve.wait_ge(max_mm, UNITS * f + i + 1)
            if i == 0 and past(f, 2):
                dve.wait_ge(maxT_mm, f - 1)
            dve.tensor_reduce(mx[:, parity, 2 * i:2 * i + 2], bank_m[:], axis=AX.X, op=ALU.max).then_inc(max_done, 1)

        def negate(f):
            dve.wait_ge(maxT_mm, f + 1)
            if past(f, 1):
                dve.wait_ge(max_in, MAX_IN * f)
            dve.tensor_scalar(nmh[:], bank_d[:, 0:P], -1.0, None, ALU.mult).then_inc(neg_hi, 1)
            dve.wait_ge(neg_hi, f + 1)
            dve.scalar_tensor_tensor(out=nml[:], in0=bank_d[:, 0:P], scalar=-1.0, in1=nmh[:].bitcast(F32),
                                     op0=ALU.mult, op1=ALU.subtract).then_inc(neg_lo, 1)

        def normalize(r):
            dve.wait_ge(den_mm, r + 1)
            if past(r, 1):
                dve.wait_ge(o_done, r)
            dve.reciprocal(rden[:], bank_d[:]).then_inc(rden_done, 1)
            dve.wait_ge(rden_done, r + 1)
            if past(r, 1):
                dve.wait_ge(ol_done, r)
            dve.wait_ge(raw_done, r + 1)
            dve.tensor_tensor(o[:], o_raw[:], rden[:], ALU.mult).then_inc(o_done, 1)

        def add_output(b, half, t):
            n = 2 * TT * b + TT * half + t
            dve.wait_ge(wo_mm, n + 1)
            if half == 0:
                dve.wait_ge(acc_in, 16 * (b + 1))
            else:
                dve.wait_ge(acc_done, n - TT + 1)
            dve.tensor_tensor(acc[:, t], bank_f[t % 2][:, 0:D], acc[:, t], ALU.add).then_inc(acc_done, 1)

        rotate(0)
        rotate(1)
        rotate(2)
        for i in range(UNITS):
            maxima(0, 0, i)
        negate(0)
        for i in range(UNITS // 2):
            maxima(0, 1, i)
        dve.wait_ge(w_hi, 4)
        lo(Wol[:].rearrange("p k c -> p (k c)"), work(0, QW), Woh[:].rearrange("p k c -> p (k c)").bitcast(F32))

        def body(b):
            for g in range(KV):
                s = 4 * b + g
                queries = not (is_last(b) and g >= 2)
                for u in range(UNITS):
                    if (m := max_unit(b, g, u)):
                        maxima(*m)
                    if g == 0 and past(b, 1) and u >= 6:
                        add_output(b - 1, 1, u - 6)
                    if g == 2 and u >= 6:
                        add_output(b, 0, u - 6)
                    if g == 1 and past(b, 1) and u < 2:
                        add_output(b - 1, 1, u + 2)
                    if g == 3 and u < 2:
                        add_output(b, 0, u + 2)
                    if u == 1 and queries:
                        rotate(rotation(b, ROT_Q[g]))
                    if u == 2 and (past(b, 1) or g > 0):
                        normalize(2 * s - 1)
                    if u == 4 and not (is_last(b) and g == KV - 1):
                        negate(s + 1)
                    if u == 6:
                        normalize(2 * s)
                    if u == UNITS - 1:
                        if g == 1 and not is_last(b):
                            rotate(rotation(b, ROT_K))

        batches(dve, body)
        normalize(2 * STEPS - 1)
        for t in range(TT):
            add_output(B - 1, 1, t)

    @block.tensor
    def _(pe):
        def after_rotation(half, r):
            pe.wait_ge(rot_mul, 4 * r + 2 + 2 * half)

        def after_values(half, b):
            pe.wait_ge(v_done, 2 * b + half + 1)

        def after_output(b, part, t):
            pe.wait_ge(acc_done, 2 * TT * b + TT * part + t + 1)

        def project(half, wh, wl):
            i = 0
            for w, part in ((wh, 0), (wl, 0), (wh, 1)):
                for k in range(DK):
                    last = pe.matmul(bank_f[half][:], w[:, k], xT[:, part, k], start=(i == 0), stop=(i == 3 * DK - 1))
                    i += 1
            last.then_inc(rope_mm, 1)

        def queries(half, g):
            project(half, Wqh[:, :, g, half], Wql[:, :, g, half])

        def keys(half):
            project(half, Wkh[:, :, half], Wkl[:, :, half])

        def values(half):
            for t in (2 * half, 2 * half + 1):
                i = 0
                for part, w in ((0, Wvh), (1, Wvh), (0, Wvl)):
                    for k in range(DK):
                        last = pe.matmul(bank_f[half][:, (t % 2) * KV * HD:(t % 2 + 1) * KV * HD],
                                         xT[:, part, k, t * P:(t + 1) * P], w[:, k],
                                         start=(i == 0), stop=(i == 3 * DK - 1))
                        i += 1
            last.then_inc(v_mm, 1)

        def output(b, half, t):
            pe.wait_ge(ol_done, PAIRS * b + OT * (half + 1))
            if t >= 2:
                after_output(b, half, t - 2)
            i = 0
            for part, w in ((oh, Woh), (ol, Woh), (oh, Wol)):
                for q in range(OT):
                    last = pe.matmul(bank_f[t % 2][:, 0:D], part[:, q, t * P:(t + 1) * P], w[:, OT * half + q],
                                     start=(i == 0), stop=(i == 3 * OT - 1))
                    i += 1
            last.then_inc(wo_mm, 1)

        def maxima(b, g, i):
            f = 4 * b + g
            if i == 0:
                pe.wait_ge(q1_in[g], Q1_IN * (b + 1))
                pe.wait_ge(k_in[g], K_IN * (b + 1))
            if past(f, 1) or i > 0:
                pe.wait_ge(max_done, UNITS * f + i)
            h = i // 2
            for j in range(2):
                t = 2 * (i % 2) + j
                last = pe.matmul(bank_m[:, j], q1[0:ROW_MAX, g, h, t * P:(t + 1) * P], k1[0:ROW_MAX, g],
                                 start=True, stop=True)
            last.then_inc(max_mm, 1)

        def transpose_maxima(f, parity):
            pe.wait_ge(max_done, UNITS * (f + 1))
            if past(f, 2):
                pe.wait_ge(rden_done, 2 * (f - 1))
            if past(f, 1):
                pe.wait_ge(neg_lo, f)
            pe.transpose(bank_d[:, 0:P], mx[:, parity], ident[:]).then_inc(maxT_mm, 1)

        def scores(b, g, u):
            s, kt = 4 * b + g, u % TT
            if u == 0:
                pe.wait_ge(max_in, MAX_IN * (s + 1))
                pe.wait_ge(q2_in[g % 2], Q2_IN * (2 * b + g // 2 + 1))
            if past(b, 1) or g > 0 or u > 0:
                pe.wait_ge(exp_done, UNITS * s + u)
            for j in range(2):
                h = 2 * (u // TT) + j
                pe.matmul(bank_s[:, j], k1[0:ROWS, g, kt * P:(kt + 1) * P], q1[0:ROWS, g, h], start=True, stop=False)
                last = pe.matmul(bank_s[:, j], k2[:, g, kt * P:(kt + 1) * P], q2[:, g % 2, h], start=False, stop=True)
            last.then_inc(score_mm, 1)

        def weighted_values(b, g, u):
            s = 4 * b + g
            kt, r = u % TT, 2 * s + u // TT
            pe.wait_ge(exp_done, UNITS * s + u + 1)
            if u == 0:
                pe.wait_ge(v_in[g], V_IN * (b + 1))
            if kt == 0 and past(r, 1):
                pe.wait_ge(raw_done, r)
            for j in range(2):
                last = pe.matmul(bank_o[j * HD:(j + 1) * HD], v[:, g, kt], p[:, kt, j], start=(kt == 0), stop=(kt == TT - 1))
            last.then_inc(pv_mm, 1)

        def row_sums(r, transposed):
            pe.wait_ge(psum_done, 3 * (r + 1))
            if past(r, 1):
                pe.wait_ge(rden_done, r)
            if transposed is not None:
                pe.wait_ge(neg_lo, transposed + 1)
            for j in range(2):
                last = pe.matmul(bank_d[j * HD:(j + 1) * HD], ones[:], psum[:, j], start=True, stop=True)
            last.then_inc(den_mm, 1)

        pe.wait_ge(w_lo, 3)
        pe.wait_ge(xt_in, 16)
        pe.wait_ge(mem_set, 2)
        pe.wait_ge(c_in, 5 * 16)
        for half in range(2):
            keys(half)
        for g in range(2):
            for half in range(2):
                after_rotation(half, g)
                queries(half, g)
        for half in range(2):
            after_rotation(half, 2)
            values(half)
        pe.wait_ge(rows_set, 2 * KV)
        for i in range(UNITS):
            maxima(0, 0, i)
        transpose_maxima(0, 0)
        for i in range(UNITS // 2):
            maxima(0, 1, i)

        def body(b):
            for g in range(KV):
                s = 4 * b + g
                nxt = not is_last(b)
                for u in range(UNITS):
                    scores(b, g, u)
                    if (m := max_unit(b, g, u)):
                        maxima(*m)
                    if u == 4 and not (is_last(b) and g == KV - 1):
                        transpose_maxima(s + 1, (g + 1) % 2)
                    if u < 2 and (g < 2 or nxt):
                        if g == 0:
                            if past(b, 1):
                                after_rotation(u, rotation(b, 0) - 1)
                            else:
                                after_values(u, 0)
                        elif g == 1:
                            if past(b, 1):
                                after_output(b - 1, 1, 2 + u)
                            else:
                                after_rotation(u, rotation(b, 0))
                        elif g == 2:
                            after_rotation(u, rotation(b, ROT_K))
                        else:
                            after_output(b, 0, 2 + u)
                        queries(u, (g + 2) % KV)
                    if g == 0 and past(b, 1):
                        if u == 5:
                            after_rotation(0, rotation(b, 0))
                            output(b - 1, 1, 0)
                        if u == 6:
                            after_rotation(1, rotation(b, 0))
                            output(b - 1, 1, 1)
                            output(b - 1, 1, 2)
                        if u == 7:
                            output(b - 1, 1, 3)
                    if g == 1 and nxt and u in (5, 6):
                        if u == 5:
                            pe.wait_ge(xt_in, 16 * (b + 2))
                        after_rotation(u - 5, rotation(b, 1))
                        keys(u - 5)
                    if g == 2 and nxt and u == 3:
                        for half in range(2):
                            after_rotation(half, rotation(b, 3))
                            values(half)
                    if g == 2 and u >= 5:
                        if u < 7:
                            if nxt:
                                after_values(u - 5, b + 1)
                            else:
                                after_rotation(u - 5, rotation(b, 1))
                        if u == 5:
                            if isinstance(b, int) and b == 0:
                                pe.wait_ge(w_lo, 4)
                            output(b, 0, 0)
                        if u == 6:
                            output(b, 0, 1)
                            output(b, 0, 2)
                        if u == 7:
                            output(b, 0, 3)
                    if u > 0:
                        weighted_values(b, g, u - 1)
                    elif past(b, 1) or g > 0:
                        weighted_values(b if g else b - 1, (g - 1) % KV, UNITS - 1)
                    if u == 1 and (past(b, 1) or g > 0):
                        row_sums(2 * s - 1, None)
                    if u == 5:
                        row_sums(2 * s, None if is_last(b) and g == KV - 1 else s + 1)

        batches(pe, body)
        weighted_values(B - 1, KV - 1, UNITS - 1)
        row_sums(2 * STEPS - 1, None)
        for t in range(TT):
            if t < 2:
                after_output(B - 1, 0, t + 2)
            output(B - 1, 1, t)


def build_program(nc, dram):
    with ExitStack() as ctx:
        phase_one(nc, dram, ctx)
    with ExitStack() as ctx:
        phase_two(nc, dram, ctx)


def host_arrays(L0_attn_x, L0_attn_Wq, L0_attn_Wk, L0_attn_Wv, L0_attn_Wo, L0_ffn_w_router,
                L0_ffn_W1, L0_ffn_b1, L0_ffn_W2, L0_ffn_b2):
    def rows(w, k):
        return np.ascontiguousarray(w.reshape((k, P) + w.shape[1:]).swapaxes(0, 1).reshape(P, -1))

    half = HD // 2
    angle = (np.arange(L, dtype=np.float32)[:, None]
             * (np.float32(1.0) / np.float32(10000.0) ** (np.arange(0, HD, 2, dtype=np.float32) / np.float32(HD)))[None])
    slopes = np.array([2.0 ** (-(h + 1) / 2) for h in range(H)], np.float32)
    bits = slopes.view(np.uint32)
    slope_hi = ((bits + 0x800) & 0xFFFFF000).astype(np.uint32).view(np.float32)
    token = np.arange(L)
    pos = np.arange(L, dtype=np.float32)
    return {
        "x": np.ascontiguousarray(L0_attn_x),
        "Wq": rows(L0_attn_Wq.reshape(D, KV, G, 2, half).transpose(0, 1, 3, 2, 4), DK),
        "Wk": rows(L0_attn_Wk.reshape(D, KV, 2, half).transpose(0, 2, 1, 3), DK),
        "Wv": rows(L0_attn_Wv, DK),
        "Wo": rows(L0_attn_Wo, H * HD // P),
        "W1": rows(L0_ffn_W1, DK),
        "W2": rows(L0_ffn_W2, FC),
        "b1": rows(L0_ffn_b1, FC),
        "b2": np.ascontiguousarray(L0_ffn_b2.reshape(1, D)),
        "router": np.ascontiguousarray(L0_ffn_w_router.reshape(1, D)),
        "cos": np.ascontiguousarray(np.tile(np.cos(angle).T, (G, 1))),
        "sin": np.ascontiguousarray(np.tile(np.sin(angle).T, (G, 1))),
        "ident": np.eye(P, dtype=np.float32),
        "iota": np.arange(SEL, dtype=np.float32).reshape(1, SEL),
        "iotac": np.ascontiguousarray(np.arange(SEL, dtype=np.float32).reshape(RT, P).T),
        "earlier": rows((token[None, :] < token[:, None]).astype(np.float32), TT).reshape(P, TT, L),
        "slope_rows": np.stack([slope_hi, slopes - slope_hi]),
        "key_rows": np.stack([pos, pos, np.ones_like(pos), np.ones_like(pos)]),
    }


def kernel(**inputs):
    import concourse.bacc as bacc
    from concourse.bass_utils import run_bass_kernel_spmd

    nc = bacc.Bacc("TRN2", target_bir_lowering=False, num_devices=1)
    arrays = host_arrays(**{name: np.asarray(a) for name, a in inputs.items()})
    dram = {name: nc.dram_tensor("in_" + name, a.shape, mybir.dt.from_np(a.dtype), kind="ExternalInput").ap()
            for name, a in arrays.items()}
    dram["xt"] = nc.dram_tensor("scratch_xt", [B, 2, P, DK, L], F32R).ap()
    dram["res"] = nc.dram_tensor("scratch_res", [B, L, D], F32).ap()
    dram["out"] = nc.dram_tensor("out", [B, L, D], F32, kind="ExternalOutput").ap()
    build_program(nc, dram)
    result = run_bass_kernel_spmd(nc, [{"in_" + name: a for name, a in arrays.items()}], core_ids=[0])
    return result.results[0]["out"]
```

```python
import math
from contextlib import ExitStack

import numpy as np
import concourse.bass as bass
import concourse.mybir as mybir

F32 = mybir.dt.float32
F32R = mybir.dt.float32r
BF16 = mybir.dt.bfloat16
ALU = mybir.AluOpType
ACT = mybir.ActivationFunctionType
AX = mybir.AxisListType

P = 128
B, L, D = 8, 512, 256
H, KV, HD = 16, 4, 64
HALF = HD // 2
G = H // KV
F = 1024
TT = L // P
DK = D // P
FC = F // P
SEL = L // 2
RT = SEL // P
STEPS = B * KV
EPS = 1e-5
ROW_SLOPE, ROW_MAX, ROWS = HD, HD + 2, HD + 4


def past(b, n):
    return not isinstance(b, int) or b >= n


def phase_one(nc, dram, ctx):
    def sb(name, shape, dt=F32):
        return ctx.enter_context(nc.sbuf_tensor(name, shape, dt))

    def ps(name):
        return ctx.enter_context(nc.psum_tensor(name, [P, 512], F32))

    def sem(name):
        return ctx.enter_context(nc.semaphore(name))

    W1h, W1l = sb("W1h", [P, DK, F], F32R), sb("W1l", [P, DK, F], F32R)
    W2h, W2l = sb("W2h", [P, FC, D], F32R), sb("W2l", [P, FC, D], F32R)
    stage = sb("stage", [P, 2, FC * D])
    ident, iota = sb("ident", [P, P]), sb("iota", [P, SEL])
    iotac, earlier = sb("iotac", [P, RT]), sb("earlier", [P, TT, L])
    router, bias1, bias2 = sb("router", [P, D]), sb("bias1", [P, FC]), sb("bias2", [P, RT, D])
    mhalf = sb("mhalf", [P, TT])
    x, xn, res = (sb(n, [P, 2, TT, D]) for n in ("x", "xn", "res"))
    xh, xl = sb("xh", [P, 2, TT, D], F32R), sb("xl", [P, 2, TT, D], F32R)
    xTh, xTl = sb("xTh", [P, 2, DK, L], F32R), sb("xTl", [P, 2, DK, L], F32R)
    stats, both, mean = sb("stats", [P, 2, TT, 6]), sb("both", [P, 3, TT, 2]), sb("mean", [P, 2, TT])
    vare, rstd = sb("vare", [P, 2, TT]), sb("rstd", [P, 2, TT])
    score, th, wt = sb("score", [P, 2, TT]), sb("th", [P, 2, TT]), sb("wt", [P, 2, TT])
    prod = sb("prod", [P, TT, D], BF16)
    srow, cmp = sb("srow", [P, L]), sb("cmp", [P, 2, L], BF16)
    rk, rank = sb("rk", [P, 2, 2, TT]), sb("rank", [P, 2, TT])
    Gm, GT = sb("Gm", [P, 2, TT, SEL], F32R), sb("GT", [P, 2, RT, L], F32R)
    xsh, xsl = sb("xsh", [P, DK * SEL], F32R), sb("xsl", [P, DK * SEL], F32R)
    g = sb("g", [P, FC, SEL])
    gh, gl = sb("gh", [P, FC, SEL], F32R), sb("gl", [P, FC, SEL], F32R)
    y = sb("y", [P, RT * D])
    yh, yl = sb("yh", [P, RT * D], F32R), sb("yl", [P, RT * D], F32R)
    rs = sb("rs", [P, TT, D])

    bank_xt = [ps("bank_xt0"), ps("bank_xt1")]
    bank_row = ps("bank_row")
    bank_sel = [ps("bank_sel0"), ps("bank_sel1")]
    bank_h = [ps("bank_h0"), ps("bank_h1")]
    bank_y = ps("bank_y")

    w_in, c_in, x_in = sem("w_in"), sem("c_in"), sem("x_in")
    w_hi, w_lo, mh_set = sem("w_hi"), sem("w_lo"), sem("mh_set")
    bn_done, ag_done, vare_done, rstd_done = sem("bn_done"), sem("ag_done"), sem("vare_done"), sem("rstd_done")
    xn_done, xh_done, xl_done, res_done = sem("xn_done"), sem("xh_done"), sem("xl_done"), sem("res_done")
    xt_mm, xth_done, xtl_done, xt_out = sem("xt_mm"), sem("xth_done"), sem("xtl_done"), sem("xt_out")
    score_done, srow_mm, srow_done = sem("score_done"), sem("srow_mm"), sem("srow_done")
    th_done, wt_done = sem("th_done"), sem("wt_done")
    cmp_done, rank_done, rrow_mm = sem("cmp_done"), sem("rank_done"), sem("rrow_mm")
    g_done, gt_done = sem("g_done"), sem("gt_done")
    sel_mm, sel_done, h_mm, gelu_done = sem("sel_mm"), sem("sel_done"), sem("h_mm"), sem("gelu_done")
    gh_done, gl_done, y_mm, y_done = sem("gh_done"), sem("gl_done"), sem("y_mm"), sem("y_done")
    yh_done, yl_done, scat_mm, rs_done, rs_out = (
        sem("yh_done"), sem("yl_done"), sem("scat_mm"), sem("rs_done"), sem("rs_out"))

    def pipeline(eng, step):
        step(0, None, 0)
        step(1, 0, 1)
        with eng.Fori(1, B // 2) as i:
            step(2 * i, 2 * i - 1, 0)
            step(2 * i + 1, 2 * i, 1)
        step(None, B - 1, 0)

    block = ctx.enter_context(nc.Block())

    @block.sync
    def _(sp):
        def load_x(b, par):
            if past(b, 2):
                sp.wait_ge(res_done, b - 1)
            sp.dma_start(x[:, par], dram["x"][b].rearrange("(t p) d -> p t d", p=P)).then_inc(x_in, 16)

        load_x(0, 0)
        sp.dma_start(ident[:], dram["ident"]).then_inc(c_in, 16)
        sp.dma_start(router[:], dram["router"].to_broadcast([P, D])).then_inc(c_in, 16)
        sp.dma_start(iota[:], dram["iota"].to_broadcast([P, SEL])).then_inc(c_in, 16)
        sp.dma_start(iotac[:], dram["iotac"]).then_inc(c_in, 16)
        sp.dma_start(earlier[:], dram["earlier"]).then_inc(c_in, 16)
        sp.dma_start(bias1[:], dram["b1"]).then_inc(c_in, 16)
        for r in range(RT):
            sp.dma_start(bias2[:, r], dram["b2"].to_broadcast([P, D])).then_inc(c_in, 16)
        sp.dma_start(stage[:, 0], dram["W1"]).then_inc(w_in, 16)
        sp.dma_start(stage[:, 1], dram["W2"]).then_inc(w_in, 16)
        load_x(1, 1)

        def step(f, b, par):
            if f is not None:
                sp.wait_ge(xth_done, DK * (f + 1))
                sp.wait_ge(xtl_done, DK * (f + 1))
                sp.dma_start(dram["xt"][f, 0].bitcast(F32), xTh[:, par].bitcast(F32)).then_inc(xt_out, 16)
                sp.dma_start(dram["xt"][f, 1].bitcast(F32), xTl[:, par].bitcast(F32)).then_inc(xt_out, 16)
            if b is not None:
                if not isinstance(b, int) or b + 2 < B:
                    load_x_next(b, 1 - par)
                sp.wait_ge(rs_done, TT * (b + 1))
                sp.dma_start(dram["res"][b].rearrange("(t p) d -> p t d", p=P), rs[:]).then_inc(rs_out, 16)

        def load_x_next(b, par):
            load_x(b + 2, par)

        step(0, None, 0)
        step(1, 0, 1)
        with sp.Fori(1, B // 2 - 1) as i:
            step(2 * i, 2 * i - 1, 0)
            step(2 * i + 1, 2 * i, 1)
        step(B - 2, B - 3, 0)
        step(B - 1, B - 2, 1)
        step(None, B - 1, 0)
        sp.wait_ge(rs_out, 16 * B)
        sp.wait_ge(xt_out, 2 * 16 * B)

    @block.gpsimd
    def _(pool):
        pool.memset(mhalf[:], -0.5).then_inc(mh_set, 1)

        def step(f, b, par):
            if f is None:
                return
            if isinstance(f, int) and f == 0:
                pool.wait_ge(mh_set, 1)
            pool.wait_ge(vare_done, f + 1)
            pool.tensor_tensor(rstd[:, par], vare[:, par], mhalf[:], ALU.pow).then_inc(rstd_done, 1)
            pool.wait_ge(xn_done, TT * (f + 1))
            if past(f, 2):
                pool.wait_ge(rs_done, TT * (f - 1))
            pool.tensor_tensor(res[:, par], x[:, par], xn[:, par], ALU.add).then_inc(res_done, 1)
            pool.wait_ge(xh_done, f + 1)
            if past(f, 2):
                pool.wait_ge(sel_mm, 2 * (f - 1))
            pool.tensor_tensor(xl[:, par], xn[:, par], xh[:, par].bitcast(F32), ALU.subtract).then_inc(xl_done, 1)

        pipeline(pool, step)

    @block.scalar
    def _(act):
        act.wait_ge(w_in, 32)
        act.activation(W1h[:].rearrange("p k n -> p (k n)"), stage[:, 0], ACT.Copy).then_inc(w_hi, 1)
        act.activation(W2h[:].rearrange("p k n -> p (k n)"), stage[:, 1], ACT.Copy).then_inc(w_hi, 1)
        act.wait_ge(c_in, 16 * 8)

        def step(f, b, par):
            if b is not None:
                for part, dst in enumerate((xsh, xsl)):
                    act.wait_ge(sel_mm, 2 * b + part + 1)
                    if past(b, 1):
                        act.wait_ge(h_mm, FC // 2 * b)
                    act.activation(dst[:], bank_sel[part][:], ACT.Copy).then_inc(sel_done, 1)
            if f is not None:
                act.wait_ge(xn_done, TT * (f + 1))
                if past(f, 2):
                    act.wait_ge(sel_mm, 2 * (f - 1))
                act.activation(xh[:, par], xn[:, par], ACT.Copy).then_inc(xh_done, 1)
                for k in range(DK):
                    act.wait_ge(xt_mm, DK * f + k + 1)
                    if past(f, 2):
                        act.wait_ge(xt_out, 32 * (f - 1))
                    act.activation(xTh[:, par, k], bank_xt[k][:], ACT.Copy).then_inc(xth_done, 1)
            if b is not None:
                for c2 in range(FC // 2 + 1):
                    if c2 < FC // 2:
                        act.wait_ge(h_mm, FC // 2 * b + c2 + 1)
                        if past(b, 1):
                            act.wait_ge(gl_done, FC // 2 * (b - 1) + c2 + 1)
                        for c in (2 * c2, 2 * c2 + 1):
                            act.activation(g[:, c], bank_h[c2 % 2][:, (c % 2) * SEL:(c % 2 + 1) * SEL],
                                           ACT.Gelu_apprx_tanh, bias=bias1[:, c:c + 1]).then_inc(gelu_done, 1)
                    if c2 > 0:
                        act.wait_ge(gelu_done, FC * b + 2 * c2)
                        if past(b, 1):
                            act.wait_ge(y_mm, RT * b)
                        act.activation(gh[:, 2 * c2 - 2:2 * c2], g[:, 2 * c2 - 2:2 * c2], ACT.Copy).then_inc(gh_done, 1)
            if f is not None:
                act.wait_ge(srow_mm, f + 1)
                if past(f, 1):
                    act.wait_ge(cmp_done, 2 * TT * f)
                act.activation(srow[:], bank_row[:], ACT.Copy).then_inc(srow_done, 1)
                act.wait_ge(score_done, TT * (f + 1))
                if past(f, 2):
                    act.wait_ge(wt_done, f - 1)
                act.activation(th[:, par], score[:, par], ACT.Tanh, scale=0.5).then_inc(th_done, 1)
            if b is not None:
                act.wait_ge(y_done, b + 1)
                if past(b, 1):
                    act.wait_ge(scat_mm, TT * b)
                act.activation(yh[:], y[:], ACT.Copy).then_inc(yh_done, 1)

        pipeline(act, step)

    @block.vector
    def _(dve):
        dve.wait_ge(w_hi, 2)
        dve.tensor_tensor(W1l[:].rearrange("p k n -> p (k n)"), stage[:, 0],
                          W1h[:].rearrange("p k n -> p (k n)").bitcast(F32), ALU.subtract).then_inc(w_lo, 1)
        dve.tensor_tensor(W2l[:].rearrange("p k n -> p (k n)"), stage[:, 1],
                          W2h[:].rearrange("p k n -> p (k n)").bitcast(F32), ALU.subtract).then_inc(w_lo, 1)
        dve.wait_ge(c_in, 16 * 8)

        def step(f, b, par):
            if f is not None:
                dve.wait_ge(x_in, 16 * (f + 1))
                for t in range(TT):
                    dve.bn_stats(stats[:, par, t], x[:, par, t]).then_inc(bn_done, 1)
                dve.wait_ge(bn_done, TT * (f + 1))
                even, odd = stats[:, par, :, 1:3], stats[:, par, :, 4:6]
                dve.tensor_tensor(both[:, 0], even, odd, ALU.add).then_inc(ag_done, 1)
                dve.tensor_tensor(both[:, 1], even, odd, ALU.subtract).then_inc(ag_done, 1)
                dve.wait_ge(ag_done, 5 * f + 2)
                dve.tensor_scalar(mean[:, par], both[:, 0, :, 0], 0.5, None, ALU.mult).then_inc(ag_done, 1)
                dve.tensor_scalar(both[:, 2, :, 0], both[:, 0, :, 1], 1.0 / D, EPS, ALU.mult, ALU.add).then_inc(ag_done, 1)
                dve.scalar_tensor_tensor(out=both[:, 2, :, 1], in0=both[:, 1, :, 0], scalar=0.25, in1=both[:, 1, :, 0],
                                         op0=ALU.mult, op1=ALU.mult).then_inc(ag_done, 1)
                dve.wait_ge(ag_done, 5 * (f + 1))
                dve.tensor_tensor(vare[:, par], both[:, 2, :, 0], both[:, 2, :, 1], ALU.add).then_inc(vare_done, 1)
                dve.wait_ge(rstd_done, f + 1)
                if past(f, 2):
                    dve.wait_ge(xl_done, f - 1)
                    dve.wait_ge(xt_mm, DK * (f - 1))
                    dve.wait_ge(score_done, TT * (f - 1))
                for t in range(TT):
                    dve.tensor_scalar(xn[:, par, t], x[:, par, t], mean[:, par, t:t + 1], rstd[:, par, t:t + 1],
                                      ALU.subtract, ALU.mult).then_inc(xn_done, 1)
                dve.wait_ge(xn_done, TT * (f + 1))
                for t in range(TT):
                    dve.tensor_tensor_reduce(out=prod[:, t], in0=xn[:, par, t], in1=router[:], scale=1.0, scalar=0.0,
                                             op0=ALU.mult, op1=ALU.add,
                                             accum_out=score[:, par, t:t + 1]).then_inc(score_done, 1)
                for k in range(DK):
                    dve.wait_ge(xth_done, DK * f + k + 1)
                    dve.tensor_tensor(xTl[:, par, k], bank_xt[k][:], xTh[:, par, k].bitcast(F32),
                                      ALU.subtract).then_inc(xtl_done, 1)
            if b is not None:
                for c2 in range(FC // 2):
                    dve.wait_ge(gh_done, FC // 2 * b + c2 + 1)
                    dve.tensor_tensor(gl[:, 2 * c2:2 * c2 + 2], g[:, 2 * c2:2 * c2 + 2],
                                      gh[:, 2 * c2:2 * c2 + 2].bitcast(F32), ALU.subtract).then_inc(gl_done, 1)
            if f is not None:
                dve.wait_ge(srow_done, f + 1)
                for t in range(TT):
                    for part in range(2):
                        n = 2 * TT * f + 2 * t + part
                        if past(n, 2):
                            dve.wait_ge(cmp_done, n - 1)
                        own = score[:, par, t:t + 1]
                        if part == 0:
                            dve.tensor_scalar(cmp[:, part], srow[:], own, None, ALU.is_gt, ALU.add,
                                              accum_out=rk[:, par, 0, t:t + 1]).then_inc(cmp_done, 1)
                        else:
                            dve.scalar_tensor_tensor(out=cmp[:, part], in0=srow[:], scalar=own, in1=earlier[:, t],
                                                     op0=ALU.is_equal, op1=ALU.mult,
                                                     accum_out=rk[:, par, 1, t:t + 1]).then_inc(cmp_done, 1)
                dve.wait_ge(cmp_done, 2 * TT * (f + 1))
                if past(f, 2):
                    dve.wait_ge(rrow_mm, f - 1)
                dve.tensor_tensor(rank[:, par], rk[:, par, 0], rk[:, par, 1], ALU.add).then_inc(rank_done, 1)
                dve.wait_ge(th_done, f + 1)
                if past(f, 2):
                    dve.wait_ge(rs_done, TT * (f - 1))
                dve.tensor_scalar(wt[:, par], th[:, par], 0.5, 0.5, ALU.mult, ALU.add).then_inc(wt_done, 1)
            if b is not None:
                dve.wait_ge(y_mm, RT * (b + 1))
                if past(b, 1):
                    dve.wait_ge(yl_done, b)
                dve.tensor_tensor(y[:], bank_y[:], bias2[:].rearrange("p r n -> p (r n)"), ALU.add).then_inc(y_done, 1)
            if f is not None:
                dve.wait_ge(rank_done, f + 1)
                if past(f, 2):
                    dve.wait_ge(sel_mm, 2 * (f - 1))
                for t in range(TT):
                    dve.tensor_scalar(Gm[:, par, t], iota[:], rank[:, par, t:t + 1], None,
                                      ALU.is_equal).then_inc(g_done, 1)
            if b is not None:
                dve.wait_ge(yh_done, b + 1)
                dve.tensor_tensor(yl[:], y[:], yh[:].bitcast(F32), ALU.subtract).then_inc(yl_done, 1)
            if f is not None:
                dve.wait_ge(rrow_mm, f + 1)
                if past(f, 2):
                    dve.wait_ge(scat_mm, TT * (f - 1))
                for r in range(RT):
                    dve.tensor_scalar(GT[:, par, r], bank_row[:], iotac[:, r:r + 1], None,
                                      ALU.is_equal).then_inc(gt_done, 1)
            if b is not None:
                back = 1 - par
                dve.wait_ge(res_done, b + 1)
                dve.wait_ge(wt_done, b + 1)
                if past(b, 1):
                    dve.wait_ge(rs_out, 16 * b)
                for t in range(TT):
                    dve.wait_ge(scat_mm, TT * b + 2 * (t // 2) + 2)
                    dve.scalar_tensor_tensor(out=rs[:, t], in0=bank_sel[t // 2][:, (t % 2) * D:(t % 2 + 1) * D],
                                             scalar=wt[:, back, t:t + 1], in1=res[:, back, t],
                                             op0=ALU.mult, op1=ALU.add).then_inc(rs_done, 1)

        pipeline(dve, step)

    @block.tensor
    def _(pe):
        pe.wait_ge(c_in, 16 * 8)
        pe.wait_ge(w_lo, 2)

        def step(f, b, par):
            back = 1 - par
            if b is not None:
                pe.wait_ge(g_done, TT * (b + 1))
                pe.wait_ge(xl_done, b + 1)
                if past(b, 1):
                    pe.wait_ge(rs_done, TT * b)
                for part, src in enumerate((xh, xl)):
                    for k in range(DK):
                        for t in range(TT):
                            last = pe.matmul(bank_sel[part][:, k * SEL:(k + 1) * SEL],
                                             src[:, back, t, k * P:(k + 1) * P], Gm[:, back, t],
                                             start=(t == 0), stop=(t == TT - 1))
                    last.then_inc(sel_mm, 1)
            if f is not None:
                pe.wait_ge(xn_done, TT * (f + 1))
                if past(f, 1):
                    pe.wait_ge(xtl_done, DK * f)
                for k in range(DK):
                    for t in range(TT):
                        last = pe.transpose(bank_xt[k][:, t * P:(t + 1) * P], xn[:, par, t, k * P:(k + 1) * P], ident[:])
                    last.then_inc(xt_mm, 1)
            if b is not None:
                pe.wait_ge(sel_done, 2 * (b + 1))
                for c2 in range(FC // 2):
                    if past(b, 1) or c2 >= 2:
                        pe.wait_ge(gelu_done, FC * b + 2 * (c2 - 1))
                    for c in (2 * c2, 2 * c2 + 1):
                        out = bank_h[c2 % 2][:, (c % 2) * SEL:(c % 2 + 1) * SEL]
                        n = 0
                        for w, xs in ((W1h, xsh), (W1l, xsh), (W1h, xsl)):
                            for k in range(DK):
                                last = pe.matmul(out, w[:, k, c * P:(c + 1) * P], xs[:, k * SEL:(k + 1) * SEL],
                                                 start=(n == 0), stop=(n == 3 * DK - 1))
                                n += 1
                    last.then_inc(h_mm, 1)
            if f is not None:
                pe.wait_ge(score_done, TT * (f + 1))
                if past(f, 1):
                    pe.wait_ge(gt_done, RT * f)
                for t in range(TT):
                    last = pe.transpose(bank_row[:, t * P:(t + 1) * P],
                                        score[:, par, t:t + 1].to_broadcast([P, P]), ident[:])
                last.then_inc(srow_mm, 1)
            if b is not None:
                if past(b, 1):
                    pe.wait_ge(y_done, b)
                for r in range(RT):
                    n = 0
                    for c in range(FC):
                        if r == 0 and c % 2 == 0:
                            pe.wait_ge(gl_done, FC // 2 * b + c // 2 + 1)
                        for gs, w in ((gh, W2h), (gl, W2h), (gh, W2l)):
                            last = pe.matmul(bank_y[:, r * D:(r + 1) * D], gs[:, c, r * P:(r + 1) * P], w[:, c],
                                             start=(n == 0), stop=(n == 3 * FC - 1))
                            n += 1
                    last.then_inc(y_mm, 1)
            if f is not None:
                pe.wait_ge(rank_done, f + 1)
                pe.wait_ge(srow_done, f + 1)
                for t in range(TT):
                    last = pe.transpose(bank_row[:, t * P:(t + 1) * P],
                                        rank[:, par, t:t + 1].to_broadcast([P, P]), ident[:])
                last.then_inc(rrow_mm, 1)
            if b is not None:
                pe.wait_ge(yl_done, b + 1)
                pe.wait_ge(gt_done, RT * (b + 1))
                for t in range(TT):
                    n = 0
                    for r in range(RT):
                        for part in (yh, yl):
                            last = pe.matmul(bank_sel[t // 2][:, (t % 2) * D:(t % 2 + 1) * D],
                                             GT[:, back, r, t * P:(t + 1) * P], part[:, r * D:(r + 1) * D],
                                             start=(n == 0), stop=(n == 2 * RT - 1))
                            n += 1
                    last.then_inc(scat_mm, 1)

        pipeline(pe, step)


def phase_two(nc, dram, ctx):
    def sb(name, shape, dt=F32):
        return ctx.enter_context(nc.sbuf_tensor("a_" + name, shape, dt))

    def ps(name, shape):
        return ctx.enter_context(nc.psum_tensor("a_" + name, shape, F32))

    def sem(name):
        return ctx.enter_context(nc.semaphore("a_" + name))

    PAIRS = H // 2
    OT = PAIRS // 2
    UNITS = TT * G // 2
    Wqh, Wql = sb("Wqh", [P, DK, H * HD], F32R), sb("Wql", [P, DK, H * HD], F32R)
    Wkh, Wkl = sb("Wkh", [P, DK, KV * HD], F32R), sb("Wkl", [P, DK, KV * HD], F32R)
    Wvh, Wvl = sb("Wvh", [P, DK, KV * HD], F32R), sb("Wvl", [P, DK, KV * HD], F32R)
    Woh, Wol = sb("Woh", [P, PAIRS, D], F32R), sb("Wol", [P, PAIRS, D], F32R)
    cos, sin = sb("cos", [P, L]), sb("sin", [P, L])
    ident, ones = sb("ident", [P, P]), sb("ones", [P, HD])
    slopes, keyrows = sb("slopes", [P, H]), sb("keyrows", [P, L])
    xT = sb("xT", [P, 2, DK, L], F32R)
    straight, swapped = sb("straight", [P, 2, L]), sb("swapped", [P, 2, L])
    qs, ks = sb("qs", [P, 4, L], F32R), sb("ks", [P, 4, L], F32R)
    q1, q2 = sb("q1", [P, KV, G, L], F32R), sb("q2", [P, 2, G, L], F32R)
    k1, k2 = sb("k1", [P, KV, L], F32R), sb("k2", [P, KV, L], F32R)
    vs, v = sb("vs", [P, TT, KV * HD]), sb("v", [P, KV, TT, HD])
    mx = sb("mx", [P, 2, P])
    nmh, nml = sb("nmh", [P, P], F32R), sb("nml", [P, P], F32R)
    p = sb("p", [P, TT, 2, L])
    psum = sb("psum", [P, 2, L])
    rden, o_raw, o = sb("rden", [P, L]), sb("o_raw", [P, L]), sb("o", [P, L])
    oh, ol = sb("oh", [P, OT, L], F32R), sb("ol", [P, OT, L], F32R)
    acc = sb("acc", [P, TT, D])

    bank_m, bank_s = ps("bank_m", [P, 2, L]), ps("bank_s", [P, 2, L])
    bank_o, bank_d = ps("bank_o", [P, L]), ps("bank_d", [P, L])
    bank_f = [ps("bank_f0", [P, L]), ps("bank_f1", [P, L])]

    w_in, w_hi, w_lo, c_in = sem("w_in"), sem("w_hi"), sem("w_lo"), sem("c_in")
    rows_set, mem_set = sem("rows_set"), sem("mem_set")
    xt_in, acc_in = sem("xt_in"), sem("acc_in")
    rope_mm, v_mm, wo_mm = sem("rope_mm"), sem("v_mm"), sem("wo_mm")
    proj_done, swap_in, kswap_in = sem("proj_done"), sem("swap_in"), sem("kswap_in")
    rot_mul, rot_sum, rope_hi, rope_lo, v_done = (
        sem("rot_mul"), sem("rot_sum"), sem("rope_hi"), sem("rope_lo"), sem("v_done"))
    q1_in, k_in, v_in = ([sem(f"{n}{g}") for g in range(KV)] for n in ("q1_in", "k_in", "v_in"))
    q2_in, max_in = [sem(f"q2_in{n}") for n in range(2)], sem("max_in")
    max_mm, max_done, maxT_mm, neg_hi, neg_lo = (
        sem("max_mm"), sem("max_done"), sem("maxT_mm"), sem("neg_hi"), sem("neg_lo"))
    score_mm, exp_done, pv_mm, psum_done, den_mm = (
        sem("score_mm"), sem("exp_done"), sem("pv_mm"), sem("psum_done"), sem("den_mm"))
    raw_done = sem("raw_done")
    ln_done, rden_done, den_read, newton_done = sem("ln_done"), sem("rden_done"), sem("den_read"), sem("newton_done")
    o_done, oh_done, ol_done = sem("o_done"), sem("oh_done"), sem("ol_done")
    acc_done, out_done = sem("acc_done"), sem("out_done")

    SWAP_IN, Q1_IN, Q2_IN, K_IN, V_IN, MAX_IN = 16 * 4, 16 * 2, 16 * 4, 16 * 3, 16, 16 * 2

    def projected_queries(b, g):
        return 4 + 5 * b + (0, 2, 3, 4)[g]

    def projected_keys(b):
        return 4 + 5 * b + 1

    def rotated_queries(b, g):
        return projected_queries(b, g - 1) if g else 5 * b + 3

    def query_rotation(b, g):
        return rotated_queries(b, g - 1) if g else 5 * b + 2

    def key_rotation(b):
        return 0 if isinstance(b, int) and b == 0 else 5 * b

    def is_last(b):
        return isinstance(b, int) and b == B - 1

    def batches(eng, body):
        body(0)
        with eng.Fori(1, B - 1) as b:
            body(b)
        body(B - 1)

    def max_unit(b, g, u):
        ahead = g + (1 if u < UNITS // 2 else 2)
        if is_last(b) and ahead >= KV:
            return None
        return b + ahead // KV, ahead % KV, (u + UNITS // 2) % UNITS

    def work(n, size):
        return p[:].rearrange("p t h l -> p (t h l)")[:, n:n + size]

    CONSTANTS = 16 * 5
    KVW = DK * KV * HD
    QW = DK * H * HD

    block = ctx.enter_context(nc.Block())

    @block.sync
    def _(sp):
        def load_xt(b):
            sp.dma_start(xT[:].rearrange("p a k l -> p a (k l)").bitcast(F32),
                         dram["xt"][b].rearrange("a p k l -> p a (k l)").bitcast(F32)).then_inc(xt_in, 16)

        def load_acc(b):
            sp.dma_start(acc[:], dram["res"][b].rearrange("(t p) d -> p t d", p=P)).then_inc(acc_in, 16)

        def store_out(b):
            sp.wait_ge(acc_done, 2 * TT * (b + 1))
            sp.dma_start(dram["out"][b].rearrange("(t p) d -> p t d", p=P), acc[:]).then_inc(out_done, 16)

        def swap_halves(r, dst, src, done):
            for i in range(4):
                j = i ^ 1
                sp.dma_start(dst[i * HALF:(i + 1) * HALF], src[j * HALF:(j + 1) * HALF]).then_inc(done, 16)

        def swap_queries(r, before):
            sp.wait_ge(proj_done, 2 * (r + 1))
            if before is not None:
                sp.wait_ge(rot_sum, 2 * (before + 1))
            swap_halves(r, swapped[:], straight[:], swap_in)

        def swap_keys(r):
            sp.wait_ge(proj_done, 2 * (r + 1))
            swap_halves(r, ks[:, 0:2].bitcast(F32), ks[:, 2:4].bitcast(F32), kswap_in)

        def place_q1(f, g, r):
            sp.wait_ge(rope_hi, 2 * (r + 1))
            if past(f, 4):
                sp.wait_ge(score_mm, UNITS * (f - 3))
            heads = q1[:, g].rearrange("p (n j) l -> p n j l", j=2)
            for j in range(2):
                sp.dma_start(heads[0:HD, :, j].bitcast(F32),
                             qs[j * HD:(j + 1) * HD, 0:2].bitcast(F32)).then_inc(q1_in[g], 16)

        def place_k(f, g, r):
            n, j = g // 2, g % 2
            sp.wait_ge(rope_lo, 2 * r + n + 1)
            if past(f, 4):
                sp.wait_ge(score_mm, UNITS * (f - 3))
            hi, lo = ks[j * HD:(j + 1) * HD, n], ks[j * HD:(j + 1) * HD, 2 + n]
            for dst, src in ((k1[0:HD, g], hi), (k2[HD:P, g], hi), (k2[0:HD, g], lo)):
                sp.dma_start(dst.bitcast(F32), src.bitcast(F32)).then_inc(k_in[g], 16)

        def place_v(f, b, g):
            sp.wait_ge(v_done, 2 * (b + 1))
            if past(f, 4):
                sp.wait_ge(pv_mm, UNITS * (f - 3))
            sp.dma_start(v[:, g], vs[:, :, g * HD:(g + 1) * HD]).then_inc(v_in[g], 16)

        def place_q2(f, slot, r):
            if past(f, 2):
                sp.wait_ge(score_mm, UNITS * (f - 1))
            sp.wait_ge(rope_lo, 2 * (r + 1))
            heads = q2[:, slot].rearrange("p (n j) l -> p n j l", j=2)
            for part in range(2):
                for j in range(2):
                    sp.dma_start(heads[part * HD:(part + 1) * HD, :, j].bitcast(F32),
                                 qs[j * HD:(j + 1) * HD, 2 * part:2 * part + 2].bitcast(F32)).then_inc(q2_in[slot], 16)

        def place_max(f, g):
            for row, src, ready in ((ROW_MAX, nmh, neg_hi), (ROW_MAX + 1, nml, neg_lo)):
                sp.wait_ge(ready, f + 1)
                sp.dma_start(q1[row:row + 1, g].rearrange("o h (t c) -> o (h t) c", c=P).bitcast(F32),
                             src[0:G * TT, :].bitcast(F32)).then_inc(max_in, 16)

        load_xt(0)
        sp.dma_start(work(0, KVW), dram["Wk"]).then_inc(w_in, 16)
        sp.dma_start(work(QW, QW), dram["Wq"]).then_inc(w_in, 16)
        sp.dma_start(work(KVW, KVW), dram["Wv"]).then_inc(w_in, 16)
        sp.dma_start(cos[:], dram["cos"]).then_inc(c_in, 16)
        sp.dma_start(sin[:], dram["sin"]).then_inc(c_in, 16)
        sp.dma_start(ident[:], dram["ident"]).then_inc(c_in, 16)
        sp.dma_start(slopes[ROW_SLOPE:ROW_MAX, :], dram["slope_rows"]).then_inc(c_in, 16)
        sp.dma_start(keyrows[ROW_SLOPE:ROWS, :], dram["key_rows"]).then_inc(c_in, 16)
        sp.wait_ge(w_lo, 3)
        sp.dma_start(work(0, QW), dram["Wo"]).then_inc(w_in, 16)
        swap_keys(0)
        swap_queries(1, None)
        place_k(0, 0, 0)
        place_q1(0, 0, 1)
        place_q2(0, 0, 1)
        swap_queries(2, 1)
        place_k(1, 1, 0)
        place_v(0, 0, 0)
        place_v(1, 0, 1)
        place_q1(1, 1, 2)
        swap_queries(3, 2)
        load_acc(0)
        place_max(0, 0)

        def body(b):
            for g in range(KV):
                s = 4 * b + g
                ahead = not (is_last(b) and g >= 2)
                if not (is_last(b) and g == KV - 1):
                    place_q2(s + 1, (g + 1) % 2, query_rotation(b, g))
                if g < 2:
                    place_k(s + 2, g + 2, key_rotation(b))
                    place_v(s + 2, b, g + 2)
                elif ahead:
                    place_k(s + 2, g - 2, key_rotation(b + 1))
                if ahead:
                    place_q1(s + 2, (g + 2) % KV, rotated_queries(b, g))
                if g == 1 and past(b, 1):
                    store_out(b - 1)
                if g == 1 and not is_last(b):
                    swap_keys(projected_keys(b))
                if g == 0 and not is_last(b):
                    sp.wait_ge(rope_mm, 2 * (projected_queries(b, 0) + 1))
                    load_xt(b + 1)
                if not (is_last(b) and g == KV - 1):
                    place_max(s + 1, (g + 1) % KV)
                if not (is_last(b) and g >= 1):
                    swap_queries(projected_queries(b, g), rotated_queries(b, g))
                if g == 1 and past(b, 1):
                    sp.wait_ge(out_done, 16 * b)
                    load_acc(b)
                if g == KV - 1 and ahead:
                    place_v(s + 1, b + 1, 0)
                    place_v(s + 2, b + 1, 1)

        batches(sp, body)
        store_out(B - 1)
        sp.wait_ge(out_done, 16 * B)

    @block.gpsimd
    def _(pool):
        pool.memset(mx[:], 0.0).then_inc(mem_set, 1)
        pool.memset(ones[:], 1.0).then_inc(mem_set, 1)

        def lo_queries(r, n):
            pool.wait_ge(rope_hi, 2 * r + n + 1)
            pool.tensor_tensor(qs[:, 2 + n], straight[:, n], qs[:, n].bitcast(F32), ALU.subtract).then_inc(rope_lo, 1)

        def lo_keys(r, n):
            pool.wait_ge(rope_hi, 2 * r + n + 1)
            pool.tensor_tensor(ks[:, 2 + n], ks[:, 2 + n].bitcast(F32), ks[:, n].bitcast(F32),
                               ALU.subtract).then_inc(rope_lo, 1)

        def output_lo(r, slot):
            pool.wait_ge(oh_done, r + 1)
            pool.tensor_tensor(ol[:, slot], o[:], oh[:, slot].bitcast(F32), ALU.subtract).then_inc(ol_done, 1)

        for n in range(2):
            lo_keys(0, n)
        for r in (1, 2):
            for n in range(2):
                lo_queries(r, n)

        def body(b):
            for g in range(KV):
                s = 4 * b + g
                queries = not (is_last(b) and g >= 2)
                for u in range(UNITS):
                    n, kt, r = UNITS * s + u, u % TT, 2 * s + u // TT
                    if kt == 1:
                        pool.wait_ge(exp_done, n + 1)
                        if past(b, 1) or r > 0:
                            pool.wait_ge(den_mm, r)
                        pool.tensor_tensor(psum[:], p[:, 0], p[:, 1], ALU.add).then_inc(psum_done, 1)
                    elif kt > 1:
                        pool.wait_ge(exp_done, n + 1)
                        pool.wait_ge(psum_done, 3 * r + kt - 1)
                        pool.tensor_tensor(psum[:], psum[:], p[:, kt], ALU.add).then_inc(psum_done, 1)
                    if u == 0 and (past(b, 1) or g > 0):
                        output_lo(2 * s - 2, (2 * g - 2) % OT)
                    if u < 2 and g == 2 and not is_last(b):
                        lo_keys(projected_keys(b), u)
                    if u in (2, 3) and queries:
                        lo_queries(rotated_queries(b, g), u - 2)
                    if u == 4 and (past(b, 1) or g > 0):
                        output_lo(2 * s - 1, (2 * g - 1) % OT)

        batches(pool, body)
        output_lo(2 * STEPS - 2, OT - 2)
        output_lo(2 * STEPS - 1, OT - 1)

    @block.scalar
    def _(act):
        def copy_hi(dst, src, scale=1.0):
            act.activation(dst, src, ACT.Copy, scale=scale).then_inc(w_hi, 1)

        act.preload_act_table_set("natural_log_exp_and_others")
        act.wait_ge(w_in, 3 * 16)
        for w, n, size, scale in ((Wkh, 0, KVW, 1.0), (Wqh, QW, QW, HD ** -0.5), (Wvh, KVW, KVW, 1.0)):
            copy_hi(w[:].rearrange("p k c -> p (k c)"), work(n, size), scale)
        act.wait_ge(c_in, CONSTANTS)
        for g in range(KV):
            act.activation(k1[ROW_SLOPE:ROWS, g], keyrows[ROW_SLOPE:ROWS, :], ACT.Copy).then_inc(rows_set, 1)
        for g in range(KV):
            act.activation(q1[ROW_SLOPE:ROW_MAX, g],
                           slopes[ROW_SLOPE:ROW_MAX, g * G:(g + 1) * G].rearrange("p (h o) -> p h o", o=1)
                           .to_broadcast([ROW_MAX - ROW_SLOPE, G, L]), ACT.Copy).then_inc(rows_set, 1)

        def project_queries(r, before):
            for n in range(2):
                act.wait_ge(rope_mm, 2 * r + n + 1)
                if before is not None:
                    act.wait_ge(rope_lo, 2 * before + n + 1)
                act.activation(straight[:, n], bank_f[n][:], ACT.Copy).then_inc(proj_done, 1)

        def project_keys(r, b):
            if b is not None:
                for slot in range(KV):
                    act.wait_ge(k_in[slot], K_IN * (b + 1))
            for n in range(2):
                act.wait_ge(rope_mm, 2 * r + n + 1)
                act.activation(ks[:, 2 + n].bitcast(F32), bank_f[n][:], ACT.Copy).then_inc(proj_done, 1)

        def keys_hi(r, n):
            act.wait_ge(rot_sum, 2 * r + n + 1)
            act.activation(ks[:, n], ks[:, 2 + n].bitcast(F32), ACT.Copy).then_inc(rope_hi, 1)

        def queries_hi(r, b, g, n):
            if past(b, 1) or g > 0:
                placed, last = (b, g - 1) if g else (b - 1, KV - 1)
                act.wait_ge(q1_in[last], Q1_IN * (placed + 1))
                act.wait_ge(q2_in[last % 2], Q2_IN * (2 * placed + last // 2 + 1))
            act.wait_ge(rot_sum, 2 * r + n + 1)
            act.activation(qs[:, n], straight[:, n], ACT.Copy).then_inc(rope_hi, 1)

        def values(b):
            for half in range(2):
                act.wait_ge(v_mm, 2 * b + half + 1)
                if past(b, 1):
                    for g in range(KV):
                        act.wait_ge(v_in[g], V_IN * b)
                act.activation(vs[:, 2 * half:2 * half + 2].rearrange("p t d -> p (t d)"), bank_f[half][:],
                               ACT.Copy).then_inc(v_done, 1)

        def output_raw(r):
            act.wait_ge(pv_mm, TT * (r + 1))
            if past(r, 1):
                act.wait_ge(o_done, r)
            act.activation(o_raw[:], bank_o[:], ACT.Copy).then_inc(raw_done, 1)

        def invert(r):
            act.wait_ge(den_mm, r + 1)
            if past(r, 1):
                act.wait_ge(newton_done, r)
            act.activation(rden[:], bank_d[:], ACT.Ln).then_inc(ln_done, 1)
            act.wait_ge(ln_done, r + 1)
            act.activation(rden[:], rden[:], ACT.Exp, scale=-1.0).then_inc(rden_done, 1)

        def output_hi(r, slot, b, g):
            act.wait_ge(o_done, r + 1)
            if g >= 2:
                act.wait_ge(wo_mm, 2 * TT * b + TT)
            elif past(b, 1):
                act.wait_ge(wo_mm, 2 * TT * b)
            act.activation(oh[:, slot], o[:], ACT.Copy).then_inc(oh_done, 1)

        project_keys(0, None)
        project_queries(1, None)
        for n in range(2):
            keys_hi(0, n)
        for n in range(2):
            queries_hi(1, 0, 0, n)
        project_queries(2, 1)
        values(0)
        for n in range(2):
            queries_hi(2, 0, 1, n)
        project_queries(3, 2)
        act.wait_ge(w_in, 4 * 16)
        copy_hi(Woh[:].rearrange("p k c -> p (k c)"), work(0, QW))

        def body(b):
            for g in range(KV):
                s = 4 * b + g
                queries = not (is_last(b) and g >= 2)
                for u in range(UNITS):
                    n, kt, r = UNITS * s + u, u % TT, 2 * s + u // TT
                    act.wait_ge(score_mm, n + 1)
                    if past(b, 1) or n >= TT:
                        act.wait_ge(pv_mm, n - TT + 1)
                        act.wait_ge(psum_done, 3 * (r - 1) + max(kt, 1))
                    if isinstance(b, int) and b == 0 and n < 1:
                        act.wait_ge(w_lo, 4)
                    act.activation(p[:, kt], bank_s[:], ACT.Exp).then_inc(exp_done, 1)
                    if u == 0 and (past(b, 1) or g > 0):
                        output_raw(2 * s - 1)
                        output_hi(2 * s - 2, (2 * g - 2) % OT, *((b, g - 1) if g else (b - 1, KV - 1)))
                    if g == 1 and u == 3 and not is_last(b):
                        project_keys(projected_keys(b), b)
                    if g == 2 and u == 0 and not is_last(b):
                        for n in range(2):
                            keys_hi(projected_keys(b), n)
                    if u in (1, 2) and queries:
                        queries_hi(rotated_queries(b, g), b + (g + 2) // KV, (g + 2) % KV, u - 1)
                    if u == 2 and (past(b, 1) or g > 0):
                        invert(2 * s - 1)
                    if u == 4:
                        output_raw(2 * s)
                    if u == 4 and (past(b, 1) or g > 0):
                        output_hi(2 * s - 1, (2 * g - 1) % OT, *((b, g - 1) if g else (b - 1, KV - 1)))
                    if u == 3 and g == 3 and not is_last(b):
                        values(b + 1)
                    if u == 5 and not (is_last(b) and g >= 1):
                        project_queries(projected_queries(b, g), rotated_queries(b, g))
                    if u == 6:
                        invert(2 * s)

        batches(act, body)
        output_raw(2 * STEPS - 1)
        output_hi(2 * STEPS - 2, OT - 2, B - 1, KV - 1)
        invert(2 * STEPS - 1)
        output_hi(2 * STEPS - 1, OT - 1, B - 1, KV - 1)

    @block.vector
    def _(dve):
        def lo(dst, src, hi, scale=1.0):
            dve.scalar_tensor_tensor(out=dst, in0=src, scalar=scale, in1=hi, op0=ALU.mult,
                                     op1=ALU.subtract).then_inc(w_lo, 1)

        for i, (lo_part, hi_part, n, size, scale) in enumerate(
                ((Wkl, Wkh, 0, KVW, 1.0), (Wql, Wqh, QW, QW, HD ** -0.5), (Wvl, Wvh, KVW, KVW, 1.0))):
            dve.wait_ge(w_hi, i + 1)
            lo(lo_part[:].rearrange("p k c -> p (k c)"), work(n, size),
               hi_part[:].rearrange("p k c -> p (k c)").bitcast(F32), scale)
        dve.wait_ge(c_in, CONSTANTS)
        dve.wait_ge(mem_set, 1)

        def rotate(r, n, heads, halves_swapped):
            dve.tensor_tensor(heads, heads, cos[:], ALU.mult).then_inc(rot_mul, 1)
            dve.tensor_tensor(halves_swapped, halves_swapped, sin[:], ALU.mult).then_inc(rot_mul, 1)
            dve.wait_ge(rot_mul, 4 * r + 2 * n + 2)
            dve.tensor_tensor(heads, heads, halves_swapped, ALU.add).then_inc(rot_sum, 1)

        def rotate_queries(r, step, n):
            dve.wait_ge(swap_in, SWAP_IN * (step + 1))
            rotate(r, n, straight[:, n], swapped[:, n])

        def rotate_keys(r, b, n):
            dve.wait_ge(kswap_in, SWAP_IN * (b + 1))
            rotate(r, n, ks[:, 2 + n].bitcast(F32), ks[:, n].bitcast(F32))

        def maxima(b, g, i):
            f, parity = 4 * b + g, g % 2
            dve.wait_ge(max_mm, UNITS * f + i + 1)
            if i == 0 and past(f, 2):
                dve.wait_ge(maxT_mm, f - 1)
            dve.tensor_reduce(mx[:, parity, 2 * i:2 * i + 2], bank_m[:], axis=AX.X, op=ALU.max).then_inc(max_done, 1)

        def negate(f):
            dve.wait_ge(maxT_mm, f + 1)
            if past(f, 1):
                dve.wait_ge(max_in, MAX_IN * f)
            dve.tensor_scalar(nmh[:], bank_d[:, 0:P], -1.0, None, ALU.mult).then_inc(neg_hi, 1)
            dve.wait_ge(neg_hi, f + 1)
            dve.scalar_tensor_tensor(out=nml[:], in0=bank_d[:, 0:P], scalar=-1.0, in1=nmh[:].bitcast(F32),
                                     op0=ALU.mult, op1=ALU.subtract).then_inc(neg_lo, 1)

        def normalize(r):
            dve.wait_ge(rden_done, r + 1)
            if past(r, 1):
                dve.wait_ge(ol_done, r)
            dve.tensor_tensor(o[:], bank_d[:], rden[:], ALU.mult).then_inc(den_read, 1)
            dve.wait_ge(den_read, r + 1)
            dve.scalar_tensor_tensor(out=o[:], in0=o[:], scalar=-2.0, in1=rden[:], op0=ALU.add,
                                     op1=ALU.mult).then_inc(newton_done, 1)
            dve.wait_ge(newton_done, r + 1)
            dve.wait_ge(raw_done, r + 1)
            dve.scalar_tensor_tensor(out=o[:], in0=o[:], scalar=-1.0, in1=o_raw[:], op0=ALU.mult,
                                     op1=ALU.mult).then_inc(o_done, 1)

        def add_output(b, half, t):
            n = 2 * TT * b + TT * half + t
            dve.wait_ge(wo_mm, n + 1)
            if half == 0:
                dve.wait_ge(acc_in, 16 * (b + 1))
            else:
                dve.wait_ge(acc_done, n - TT + 1)
            dve.tensor_tensor(acc[:, t], bank_f[t % 2][:, 0:D], acc[:, t], ALU.add).then_inc(acc_done, 1)

        for n in range(2):
            rotate_keys(0, 0, n)
        for step in range(2):
            for n in range(2):
                rotate_queries(1 + step, step, n)
        for i in range(UNITS):
            maxima(0, 0, i)
        negate(0)
        for i in range(UNITS // 2):
            maxima(0, 1, i)
        dve.wait_ge(w_hi, 4)
        lo(Wol[:].rearrange("p k c -> p (k c)"), work(0, QW), Woh[:].rearrange("p k c -> p (k c)").bitcast(F32))

        def body(b):
            for g in range(KV):
                s = 4 * b + g
                queries = not (is_last(b) and g >= 2)
                for u in range(UNITS):
                    if (m := max_unit(b, g, u)):
                        maxima(*m)
                    if g == 0 and past(b, 1) and u >= 6:
                        add_output(b - 1, 1, u - 6)
                    if g == 2 and u >= 6:
                        add_output(b, 0, u - 6)
                    if g == 1 and past(b, 1) and u < 2:
                        add_output(b - 1, 1, u + 2)
                    if g == 3 and u < 2:
                        add_output(b, 0, u + 2)
                    if u < 2 and queries:
                        rotate_queries(rotated_queries(b, g), s + 2, u)
                    if u == 3 and (past(b, 1) or g > 0):
                        normalize(2 * s - 1)
                    if u == 4 and not (is_last(b) and g == KV - 1):
                        negate(s + 1)
                    if u in (5, 6) and g == 1 and not is_last(b):
                        rotate_keys(projected_keys(b), b + 1, u - 5)
                    if u == 7:
                        normalize(2 * s)

        batches(dve, body)
        normalize(2 * STEPS - 1)
        for t in range(TT):
            add_output(B - 1, 1, t)

    @block.tensor
    def _(pe):
        def after_projection(bank, r):
            pe.wait_ge(proj_done, 2 * r + bank + 1)

        def after_values(half, b):
            pe.wait_ge(v_done, 2 * b + half + 1)

        def after_output(b, part, t):
            pe.wait_ge(acc_done, 2 * TT * b + TT * part + t + 1)

        def project(wh, wl, head, before):
            for n in range(2):
                before(n)
                columns = slice((head + 2 * n) * HD, (head + 2 * n + 2) * HD)
                i = 0
                for w, part in ((wh, 0), (wl, 0), (wh, 1)):
                    for k in range(DK):
                        last = pe.matmul(bank_f[n][:], w[:, k, columns], xT[:, part, k],
                                         start=(i == 0), stop=(i == 3 * DK - 1))
                        i += 1
                last.then_inc(rope_mm, 1)

        def queries(g, before):
            project(Wqh, Wql, G * g, before)

        def keys(before):
            project(Wkh, Wkl, 0, before)

        def values(half):
            for t in (2 * half, 2 * half + 1):
                i = 0
                for part, w in ((0, Wvh), (1, Wvh), (0, Wvl)):
                    for k in range(DK):
                        last = pe.matmul(bank_f[half][:, (t % 2) * KV * HD:(t % 2 + 1) * KV * HD],
                                         xT[:, part, k, t * P:(t + 1) * P], w[:, k],
                                         start=(i == 0), stop=(i == 3 * DK - 1))
                        i += 1
            last.then_inc(v_mm, 1)

        def output(b, half, t):
            pe.wait_ge(ol_done, PAIRS * b + OT * (half + 1))
            if t >= 2:
                after_output(b, half, t - 2)
            i = 0
            for part, w in ((oh, Woh), (ol, Woh), (oh, Wol)):
                for q in range(OT):
                    last = pe.matmul(bank_f[t % 2][:, 0:D], part[:, q, t * P:(t + 1) * P], w[:, OT * half + q],
                                     start=(i == 0), stop=(i == 3 * OT - 1))
                    i += 1
            last.then_inc(wo_mm, 1)

        def maxima(b, g, i):
            f = 4 * b + g
            if i == 0:
                pe.wait_ge(k_in[g], K_IN * (b + 1))
                pe.wait_ge(q1_in[g], Q1_IN * (b + 1))
            if past(f, 1) or i > 0:
                pe.wait_ge(max_done, UNITS * f + i)
            h = i // 2
            for j in range(2):
                t = 2 * (i % 2) + j
                last = pe.matmul(bank_m[:, j], q1[0:ROW_MAX, g, h, t * P:(t + 1) * P], k1[0:ROW_MAX, g],
                                 start=True, stop=True)
            last.then_inc(max_mm, 1)

        def transpose_maxima(f, parity):
            pe.wait_ge(max_done, UNITS * (f + 1))
            if past(f, 2):
                pe.wait_ge(den_read, 2 * (f - 1))
            if past(f, 1):
                pe.wait_ge(neg_lo, f)
            pe.transpose(bank_d[:, 0:P], mx[:, parity], ident[:]).then_inc(maxT_mm, 1)

        def scores(b, g, u):
            s, kt = 4 * b + g, u % TT
            if u == 0:
                pe.wait_ge(max_in, MAX_IN * (s + 1))
                pe.wait_ge(q2_in[g % 2], Q2_IN * (2 * b + g // 2 + 1))
            if past(b, 1) or g > 0 or u > 0:
                pe.wait_ge(exp_done, UNITS * s + u)
            for j in range(2):
                h = 2 * (u // TT) + j
                pe.matmul(bank_s[:, j], k1[0:ROWS, g, kt * P:(kt + 1) * P], q1[0:ROWS, g, h], start=True, stop=False)
                last = pe.matmul(bank_s[:, j], k2[:, g, kt * P:(kt + 1) * P], q2[:, g % 2, h], start=False, stop=True)
            last.then_inc(score_mm, 1)

        def weighted_values(b, g, u):
            s = 4 * b + g
            kt, r = u % TT, 2 * s + u // TT
            pe.wait_ge(exp_done, UNITS * s + u + 1)
            if u == 0:
                pe.wait_ge(v_in[g], V_IN * (b + 1))
            if kt == 0 and past(r, 1):
                pe.wait_ge(raw_done, r)
            for j in range(2):
                last = pe.matmul(bank_o[j * HD:(j + 1) * HD], v[:, g, kt], p[:, kt, j], start=(kt == 0), stop=(kt == TT - 1))
            last.then_inc(pv_mm, 1)

        def row_sums(r, transposed):
            pe.wait_ge(psum_done, 3 * (r + 1))
            if past(r, 1):
                pe.wait_ge(den_read, r)
            if transposed is not None:
                pe.wait_ge(neg_lo, transposed + 1)
            for j in range(2):
                last = pe.matmul(bank_d[j * HD:(j + 1) * HD], ones[:], psum[:, j], start=True, stop=True)
            last.then_inc(den_mm, 1)

        pe.wait_ge(w_lo, 3)
        pe.wait_ge(xt_in, 16)
        pe.wait_ge(mem_set, 2)
        pe.wait_ge(c_in, CONSTANTS)
        keys(lambda bank: None)
        for g in range(2):
            queries(g, lambda bank: after_projection(bank, g))
        for half in range(2):
            after_projection(half, 2)
            values(half)
        queries(2, lambda bank: after_values(bank, 0))
        pe.wait_ge(rows_set, 2 * KV)
        for i in range(UNITS):
            maxima(0, 0, i)
        transpose_maxima(0, 0)
        for i in range(UNITS // 2):
            maxima(0, 1, i)

        OUTPUTS = {5: (0,), 6: (1,), 7: (2, 3)}

        def before_keys(b, bank):
            if past(b, 1):
                after_output(b - 1, 1, 2 + bank)
            else:
                after_projection(bank, projected_queries(b, 0))

        def before_queries(b, g, bank):
            if g < 3:
                after_projection(bank, projected_queries(b, g) - 1)
            else:
                after_values(bank, b + 1)

        def body(b):
            for g in range(KV):
                s = 4 * b + g
                nxt = not is_last(b)
                for u in range(UNITS):
                    scores(b, g, u)
                    if (m := max_unit(b, g, u)):
                        maxima(*m)
                    if u == 2 and g == 1 and nxt:
                        pe.wait_ge(xt_in, 16 * (b + 2))
                        keys(lambda bank: before_keys(b, bank))
                    if u == 2 and g == 3 and nxt:
                        for half in range(2):
                            after_output(b, 0, 2 + half)
                            values(half)
                    if u == 4 and (nxt or g == 0):
                        queries((g + 3) % KV, lambda bank: before_queries(b, g, bank))
                    if g == 0 and past(b, 1) and u >= 5:
                        if u < 7:
                            after_projection(u - 5, projected_queries(b, 0))
                        for t in OUTPUTS[u]:
                            output(b - 1, 1, t)
                    if g == 2 and u >= 5:
                        if u < 7:
                            if nxt:
                                after_projection(u - 5, projected_queries(b, 2))
                            else:
                                after_output(b - 1, 1, u - 3)
                        if isinstance(b, int) and b == 0 and u == 5:
                            pe.wait_ge(w_lo, 4)
                        for t in OUTPUTS[u]:
                            output(b, 0, t)
                    if u > 0:
                        weighted_values(b, g, u - 1)
                    elif past(b, 1) or g > 0:
                        weighted_values(b if g else b - 1, (g - 1) % KV, UNITS - 1)
                    if u == 4 and not (is_last(b) and g == KV - 1):
                        transpose_maxima(s + 1, (g + 1) % 2)
                    if u == 1 and (past(b, 1) or g > 0):
                        row_sums(2 * s - 1, None)
                    if u == 5:
                        row_sums(2 * s, None if is_last(b) and g == KV - 1 else s + 1)

        batches(pe, body)
        weighted_values(B - 1, KV - 1, UNITS - 1)
        row_sums(2 * STEPS - 1, None)
        for t in range(TT):
            if t < 2:
                after_output(B - 1, 0, t + 2)
            output(B - 1, 1, t)


def build_program(nc, dram):
    with ExitStack() as ctx:
        phase_one(nc, dram, ctx)
    with ExitStack() as ctx:
        phase_two(nc, dram, ctx)


def host_arrays(L0_attn_x, L0_attn_Wq, L0_attn_Wk, L0_attn_Wv, L0_attn_Wo, L0_ffn_w_router,
                L0_ffn_W1, L0_ffn_b1, L0_ffn_W2, L0_ffn_b2):
    def rows(w, k):
        return np.ascontiguousarray(w.reshape((k, P) + w.shape[1:]).swapaxes(0, 1).reshape(P, -1))

    angle = (np.arange(L, dtype=np.float32)[:, None]
             * (np.float32(1.0) / np.float32(10000.0) ** (np.arange(0, HD, 2, dtype=np.float32) / np.float32(HD)))[None])
    slopes = np.array([2.0 ** (-(h + 1) / 2) for h in range(H)], np.float32)
    bits = slopes.view(np.uint32)
    slope_hi = ((bits + 0x800) & 0xFFFFF000).astype(np.uint32).view(np.float32)
    token = np.arange(L)
    pos = np.arange(L, dtype=np.float32)
    return {
        "x": np.ascontiguousarray(L0_attn_x),
        "Wq": rows(L0_attn_Wq, DK),
        "Wk": rows(L0_attn_Wk, DK),
        "Wv": rows(L0_attn_Wv, DK),
        "Wo": rows(L0_attn_Wo, H * HD // P),
        "W1": rows(L0_ffn_W1, DK),
        "W2": rows(L0_ffn_W2, FC),
        "b1": rows(L0_ffn_b1, FC),
        "b2": np.ascontiguousarray(L0_ffn_b2.reshape(1, D)),
        "router": np.ascontiguousarray(L0_ffn_w_router.reshape(1, D)),
        "cos": np.ascontiguousarray(np.tile(np.cos(angle).T, (4, 1))),
        "sin": np.ascontiguousarray(np.tile(np.concatenate([-np.sin(angle).T, np.sin(angle).T]), (2, 1))),
        "ident": np.eye(P, dtype=np.float32),
        "iota": np.arange(SEL, dtype=np.float32).reshape(1, SEL),
        "iotac": np.ascontiguousarray(np.arange(SEL, dtype=np.float32).reshape(RT, P).T),
        "earlier": rows((token[None, :] < token[:, None]).astype(np.float32), TT).reshape(P, TT, L),
        "slope_rows": np.stack([slope_hi, slopes - slope_hi]),
        "key_rows": np.stack([pos, pos, np.ones_like(pos), np.ones_like(pos)]),
    }


def kernel(**inputs):
    import concourse.bacc as bacc
    from concourse.bass_utils import run_bass_kernel_spmd

    nc = bacc.Bacc("TRN2", target_bir_lowering=False, num_devices=1)
    arrays = host_arrays(**{name: np.asarray(a) for name, a in inputs.items()})
    dram = {name: nc.dram_tensor("in_" + name, a.shape, mybir.dt.from_np(a.dtype), kind="ExternalInput").ap()
            for name, a in arrays.items()}
    dram["xt"] = nc.dram_tensor("scratch_xt", [B, 2, P, DK, L], F32R).ap()
    dram["res"] = nc.dram_tensor("scratch_res", [B, L, D], F32).ap()
    dram["out"] = nc.dram_tensor("out", [B, L, D], F32, kind="ExternalOutput").ap()
    build_program(nc, dram)
    result = run_bass_kernel_spmd(nc, [{"in_" + name: a for name, a in arrays.items()}], core_ids=[0])
    return result.results[0]["out"]
```

```python
from contextlib import ExitStack

import numpy as np
import concourse.mybir as mybir

F32 = mybir.dt.float32
F32R = mybir.dt.float32r
BF16 = mybir.dt.bfloat16
ALU = mybir.AluOpType
ACT = mybir.ActivationFunctionType
AX = mybir.AxisListType

P = 128
B, L, D = 8, 512, 256
H, KV, HD = 16, 4, 64
HALF = HD // 2
G = H // KV
F = 1024
TT = L // P
DK = D // P
FC = F // P
SEL = L // 2
RT = SEL // P
STEPS = B * KV
EPS = 1e-5
ROW_SLOPE, ROW_MAX, ROWS = HD, HD + 2, HD + 4


def past(b, n):
    return not isinstance(b, int) or b >= n


class Kept:
    def __init__(self, nc, ctx):
        def sb(name, shape, dt=F32):
            return ctx.enter_context(nc.sbuf_tensor("kept_" + name, shape, dt))

        self.ident = sb("ident", [P, P])
        self.cos, self.sin = sb("cos", [P, L]), sb("sin", [P, L])
        self.xT = sb("xT", [P, 2, DK, L], F32R)
        self.acc = sb("acc", [P, TT, D])
        self.xt_in, self.rs_out = (ctx.enter_context(nc.semaphore(n)) for n in ("xt_in", "rs_out"))
        self.Wqh, self.Wql = sb("Wqh", [P, DK, H * HD], F32R), sb("Wql", [P, DK, H * HD], F32R)
        self.Wkh, self.Wkl = sb("Wkh", [P, DK, KV * HD], F32R), sb("Wkl", [P, DK, KV * HD], F32R)
        self.Wvh, self.Wvl = sb("Wvh", [P, DK, KV * HD], F32R), sb("Wvl", [P, DK, KV * HD], F32R)


def load_xt(sp, dram, kept, b):
    sp.dma_start(kept.xT[:].rearrange("p a k l -> p a (k l)").bitcast(F32),
                 dram["xt"][b].rearrange("a p k l -> p a (k l)").bitcast(F32)).then_inc(kept.xt_in, 16)


def flat(w):
    return w[:].rearrange("p k c -> p (k c)")


def phase_one(nc, dram, ctx, kept):
    def sb(name, shape, dt=F32):
        return ctx.enter_context(nc.sbuf_tensor(name, shape, dt))

    def ps(name):
        return ctx.enter_context(nc.psum_tensor(name, [P, 512], F32))

    def sem(name):
        return ctx.enter_context(nc.semaphore(name))

    W1h, W1l = sb("W1h", [P, DK, F], F32R), sb("W1l", [P, DK, F], F32R)
    W2h, W2l = sb("W2h", [P, FC, D], F32R), sb("W2l", [P, FC, D], F32R)
    stage = sb("stage", [P, 2, FC * D])
    ident, iota, iotac = kept.ident, sb("iota", [P, SEL]), sb("iotac", [P, RT])
    earlier = sb("earlier", [P, L])
    router, bias1, bias2 = sb("router", [P, D]), sb("bias1", [P, FC]), sb("bias2", [P, D])
    mhalf = sb("mhalf", [P, TT])
    x, xn, res = (sb(n, [P, 2, TT, D]) for n in ("x", "xn", "res"))
    xh, xl = sb("xh", [P, 2, TT, D], F32R), sb("xl", [P, 2, TT, D], F32R)
    xTh, xTl = sb("xTh", [P, 2, DK, L], F32R), sb("xTl", [P, 2, DK, L], F32R)
    stats, both, mean = sb("stats", [P, 2, TT, 6]), sb("both", [P, 3, TT, 2]), sb("mean", [P, 2, TT])
    vare, rstd = sb("vare", [P, 2, TT]), sb("rstd", [P, 2, TT])
    score, th, wt = sb("score", [P, 2, TT]), sb("th", [P, 2, TT]), sb("wt", [P, 2, TT])
    prod = sb("prod", [P, TT, D], BF16)
    srow, cmp = sb("srow", [P, L]), sb("cmp", [P, 2, L], BF16)
    rk, rank = sb("rk", [P, 2, 2, TT]), sb("rank", [P, 2, TT])
    Gm, GT = sb("Gm", [P, 2, TT, SEL], F32R), sb("GT", [P, 2, RT, L], F32R)
    xsh, xsl = sb("xsh", [P, DK * SEL], F32R), sb("xsl", [P, DK * SEL], F32R)
    g = sb("g", [P, FC, SEL])
    gh, gl = sb("gh", [P, FC, SEL], F32R), sb("gl", [P, FC, SEL], F32R)
    y = sb("y", [P, RT, D])
    yh, yl = sb("yh", [P, RT, D], F32R), sb("yl", [P, RT, D], F32R)
    rs, rs_out = kept.acc, kept.rs_out

    bank_xt = [ps("bank_xt0"), ps("bank_xt1")]
    bank_row = ps("bank_row")
    bank_sel = [ps("bank_sel0"), ps("bank_sel1")]
    bank_h = [ps("bank_h0"), ps("bank_h1")]
    bank_y = [ps("bank_y"), bank_h[0]]
    bank_back = [bank_h[1], bank_y[0]]

    w_in, c_in, late_in = sem("w_in"), sem("c_in"), sem("late_in")
    x_in = [sem("x_in0"), sem("x_in1")]
    attn_in, attn_hi, attn_lo = sem("attn_in"), sem("attn_hi"), sem("attn_lo")
    w_hi, w_lo, mem_set = sem("w_hi"), sem("w_lo"), sem("mem_set")
    CONSTANTS = 16 * 5
    bn_done, ag_done, vare_done, rstd_done = sem("bn_done"), sem("ag_done"), sem("vare_done"), sem("rstd_done")
    xn_done, xh_done, xl_done, res_done = sem("xn_done"), sem("xh_done"), sem("xl_done"), sem("res_done")
    xt_mm, xth_done, xtl_done = sem("xt_mm"), sem("xth_done"), sem("xtl_done")
    xt_out = [sem("xt_out0"), sem("xt_out1")]
    score_done, srow_mm, srow_done = sem("score_done"), sem("srow_mm"), sem("srow_done")
    th_done, wt_done = sem("th_done"), sem("wt_done")
    cmp_done, rank_done, rrow_mm = sem("cmp_done"), sem("rank_done"), sem("rrow_mm")
    g_done, gt_done = sem("g_done"), sem("gt_done")
    sel_mm, sel_done, h_mm, gelu_done = sem("sel_mm"), sem("sel_done"), sem("h_mm"), sem("gelu_done")
    gh_done, gl_done, y_mm, y_done = sem("gh_done"), sem("gl_done"), sem("y_mm"), sem("y_done")
    yh_done, yl_done, scat_mm, rs_done = sem("yh_done"), sem("yl_done"), sem("scat_mm"), sem("rs_done")

    def pipeline(eng, step, after=None):
        for i in range(3):
            step(i, i - 1 if i > 0 else None, i - 2 if i > 1 else None, (i - 1) % 2)
            if after:
                after(i)
        with eng.Fori(1, B // 2 - 1) as i:
            step(2 * i + 1, 2 * i, 2 * i - 1, 0)
            step(2 * i + 2, 2 * i + 1, 2 * i, 1)
        step(B - 1, B - 2, B - 3, 0)
        step(None, B - 1, B - 2, 1)
        step(None, None, B - 1, 0)

    KVW, QW = DK * KV * HD, DK * H * HD
    ATTENTION = ((kept.Wkh, kept.Wkl, 0, KVW, 1.0, "Wk"), (kept.Wvh, kept.Wvl, KVW, KVW, 1.0, "Wv"),
                 (kept.Wqh, kept.Wql, FC * D, QW, HD ** -0.5, "Wq"))

    def staged(n, size):
        return stage[:].rearrange("p a n -> p (a n)")[:, n:n + size]

    block = ctx.enter_context(nc.Block())

    @block.sync
    def _(sp):
        def load_x(b, par):
            if past(b, 2):
                sp.wait_ge(res_done, b - 1)
            sp.dma_start(x[:, par], dram["x"][b].rearrange("(t p) d -> p t d", p=P)).then_inc(x_in[par], 16)

        load_x(0, 0)
        sp.dma_start(ident[:], dram["ident"]).then_inc(c_in, 16)
        sp.dma_start(router[:], dram["router"].to_broadcast([P, D])).then_inc(c_in, 16)
        sp.dma_start(iota[:], dram["iota"].to_broadcast([P, SEL])).then_inc(c_in, 16)
        sp.dma_start(iotac[:], dram["iotac"]).then_inc(c_in, 16)
        sp.dma_start(earlier[:, (TT - 1) * P:TT * P], dram["earlier"]).then_inc(c_in, 16)
        load_x(1, 1)
        for n, w in enumerate(("W1", "W2")):
            sp.dma_start(stage[:, n], dram[w]).then_inc(w_in, 16)
        sp.dma_start(bias1[:], dram["b1"]).then_inc(late_in, 16)
        sp.dma_start(bias2[:], dram["b2"].to_broadcast([P, D])).then_inc(late_in, 16)
        sp.dma_start(kept.cos[:], dram["cos"]).then_inc(late_in, 16)
        sp.dma_start(kept.sin[:], dram["sin"]).then_inc(late_in, 16)

        def step(n, f, b, par):
            if f is not None:
                if not isinstance(f, int) or f + 2 < B:
                    load_x(f + 2, par)
                sp.wait_ge(xth_done, DK * (f + 1))
                sp.wait_ge(xtl_done, DK * (f + 1))
                sp.dma_start(dram["xt"][f, 0].bitcast(F32), xTh[:, par].bitcast(F32)).then_inc(xt_out[par], 16)
                sp.dma_start(dram["xt"][f, 1].bitcast(F32), xTl[:, par].bitcast(F32)).then_inc(xt_out[par], 16)
            if b is not None:
                sp.wait_ge(rs_done, TT * (b + 1))
                sp.dma_start(dram["res"][b].rearrange("(t p) d -> p t d", p=P), rs[:]).then_inc(rs_out, 16)

        def attention_weights(i):
            if i == 1:
                sp.wait_ge(w_lo, 2)
                for _, _, n, size, _, name in ATTENTION:
                    sp.dma_start(staged(n, size), dram[name]).then_inc(attn_in, 16)
            if i == 2:
                sp.wait_ge(xt_out[0], 2 * 16)
                load_xt(sp, dram, kept, 0)

        pipeline(sp, step, attention_weights)
        for done in xt_out:
            sp.wait_ge(done, 16 * B)

    @block.gpsimd
    def _(pool):
        pool.memset(mhalf[:], -0.5).then_inc(mem_set, 1)
        pool.memset(earlier[:, 0:(TT - 1) * P], 1.0).then_inc(mem_set, 1)

        def step(n, f, b, par):
            if f is not None:
                pool.wait_ge(xn_done, TT * (f + 1))
                if past(f, 2):
                    pool.wait_ge(rs_done, TT * (f - 1))
                pool.tensor_tensor(res[:, par], x[:, par], xn[:, par], ALU.add).then_inc(res_done, 1)
            if n is not None:
                if isinstance(n, int) and n == 0:
                    pool.wait_ge(mem_set, 1)
                pool.wait_ge(vare_done, n + 1)
                pool.tensor_tensor(rstd[:, 1 - par], vare[:, 1 - par], mhalf[:], ALU.pow).then_inc(rstd_done, 1)
            if f is not None:
                pool.wait_ge(xh_done, f + 1)
                if past(f, 2):
                    pool.wait_ge(sel_mm, 2 * (f - 1))
                pool.tensor_tensor(xl[:, par], xn[:, par], xh[:, par].bitcast(F32), ALU.subtract).then_inc(xl_done, 1)
            if b is not None:
                for c2 in range(FC // 2):
                    pool.wait_ge(gh_done, FC // 2 * b + c2 + 1)
                    pool.tensor_tensor(gl[:, 2 * c2:2 * c2 + 2], g[:, 2 * c2:2 * c2 + 2],
                                       gh[:, 2 * c2:2 * c2 + 2].bitcast(F32), ALU.subtract).then_inc(gl_done, 1)

        def weights(i):
            if i == 1:
                for n, (lo, hi) in enumerate(((W1l, W1h), (W2l, W2h))):
                    pool.wait_ge(w_hi, n + 1)
                    pool.tensor_tensor(flat(lo), stage[:, n], flat(hi).bitcast(F32), ALU.subtract).then_inc(w_lo, 1)

        pipeline(pool, step, weights)

    @block.scalar
    def _(act):
        def step(n, f, b, par):
            if f is not None:
                for k in range(DK):
                    act.wait_ge(xt_mm, DK * f + k + 1)
                    if past(f, 2):
                        act.wait_ge(xt_out[par], 16 * (f - par))
                    act.activation(xTh[:, par, k], bank_xt[k][:], ACT.Copy).then_inc(xth_done, 1)
            if b is not None:
                for part, dst in enumerate((xsh, xsl)):
                    act.wait_ge(sel_mm, 2 * b + part + 1)
                    if past(b, 1):
                        act.wait_ge(h_mm, FC // 2 * b)
                    act.activation(dst[:], bank_sel[part][:], ACT.Copy).then_inc(sel_done, 1)
            if f is not None:
                act.wait_ge(srow_mm, f + 1)
                if past(f, 1):
                    act.wait_ge(cmp_done, 2 * TT * f)
                act.activation(srow[:], bank_row[:], ACT.Copy).then_inc(srow_done, 1)
                act.wait_ge(score_done, TT * (f + 1))
                if past(f, 2):
                    act.wait_ge(wt_done, f - 1)
                act.activation(th[:, par], score[:, par], ACT.Tanh, scale=0.5).then_inc(th_done, 1)
                act.wait_ge(xn_done, TT * (f + 1))
                if past(f, 2):
                    act.wait_ge(sel_mm, 2 * (f - 1))
                act.activation(xh[:, par], xn[:, par], ACT.Copy).then_inc(xh_done, 1)
            if b is not None:
                for c2 in range(FC // 2 + 1):
                    if c2 < FC // 2:
                        act.wait_ge(h_mm, FC // 2 * b + c2 + 1)
                        if past(b, 1):
                            act.wait_ge(gl_done, FC // 2 * (b - 1) + c2 + 1)
                        for c in (2 * c2, 2 * c2 + 1):
                            act.activation(g[:, c], bank_h[c2 % 2][:, (c % 2) * SEL:(c % 2 + 1) * SEL],
                                           ACT.Gelu_apprx_tanh, bias=bias1[:, c:c + 1]).then_inc(gelu_done, 1)
                    if c2 > 0:
                        act.wait_ge(gelu_done, FC * b + 2 * c2)
                        if past(b, 1):
                            act.wait_ge(y_mm, RT * b)
                        act.activation(gh[:, 2 * c2 - 2:2 * c2], g[:, 2 * c2 - 2:2 * c2], ACT.Copy).then_inc(gh_done, 1)
            if b is not None:
                for r in range(RT):
                    act.wait_ge(y_done, RT * b + r + 1)
                    if past(b, 1):
                        act.wait_ge(scat_mm, TT * b)
                    act.activation(yh[:, r], y[:, r], ACT.Copy).then_inc(yh_done, 1)

        def weights(i):
            if i == 1:
                act.wait_ge(late_in, 4 * 16)
                for n, w in enumerate((W1h, W2h)):
                    act.wait_ge(w_in, 32)
                    act.activation(flat(w), stage[:, n], ACT.Copy).then_inc(w_hi, 1)
            if i == 2:
                act.wait_ge(attn_in, 3 * 16)
                for hi, _, at, size, scale, _ in ATTENTION:
                    act.activation(flat(hi), staged(at, size), ACT.Copy, scale=scale).then_inc(attn_hi, 1)

        pipeline(act, step, weights)

    @block.vector
    def _(dve):
        def statistics(n, slot):
            dve.wait_ge(x_in[slot], 8 * (n - slot) + 16)
            for t in range(TT):
                dve.bn_stats(stats[:, slot, t], x[:, slot, t]).then_inc(bn_done, 1)
            dve.wait_ge(bn_done, TT * (n + 1))
            even, odd = stats[:, slot, :, 1:3], stats[:, slot, :, 4:6]
            dve.tensor_tensor(both[:, 0], even, odd, ALU.add).then_inc(ag_done, 1)
            dve.tensor_tensor(both[:, 1], even, odd, ALU.subtract).then_inc(ag_done, 1)
            dve.wait_ge(ag_done, 5 * n + 2)
            dve.tensor_scalar(mean[:, slot], both[:, 0, :, 0], 0.5, None, ALU.mult).then_inc(ag_done, 1)
            dve.tensor_scalar(both[:, 2, :, 0], both[:, 0, :, 1], 1.0 / D, EPS, ALU.mult, ALU.add).then_inc(ag_done, 1)
            dve.scalar_tensor_tensor(out=both[:, 2, :, 1], in0=both[:, 1, :, 0], scalar=0.25, in1=both[:, 1, :, 0],
                                     op0=ALU.mult, op1=ALU.mult).then_inc(ag_done, 1)
            dve.wait_ge(ag_done, 5 * (n + 1))
            dve.tensor_tensor(vare[:, slot], both[:, 2, :, 0], both[:, 2, :, 1], ALU.add).then_inc(vare_done, 1)

        def normalize(n, slot):
            dve.wait_ge(rstd_done, n + 1)
            if past(n, 2):
                dve.wait_ge(xl_done, n - 1)
                dve.wait_ge(xt_mm, DK * (n - 1))
                dve.wait_ge(score_done, TT * (n - 1))
            for t in range(TT):
                dve.tensor_scalar(xn[:, slot, t], x[:, slot, t], mean[:, slot, t:t + 1], rstd[:, slot, t:t + 1],
                                  ALU.subtract, ALU.mult).then_inc(xn_done, 1)

        def step(n, f, b, par):
            if n is not None:
                statistics(n, 1 - par)
            if f is not None:
                for k in range(DK):
                    dve.wait_ge(xth_done, DK * f + k + 1)
                    dve.tensor_tensor(xTl[:, par, k], bank_xt[k][:], xTh[:, par, k].bitcast(F32),
                                      ALU.subtract).then_inc(xtl_done, 1)
                dve.wait_ge(srow_done, f + 1)
                for t in range(TT):
                    for part in range(2):
                        i = 2 * TT * f + 2 * t + part
                        if past(i, 2):
                            dve.wait_ge(cmp_done, i - 1)
                        own = score[:, par, t:t + 1]
                        if part == 0:
                            dve.tensor_scalar(cmp[:, part], srow[:], own, None, ALU.is_gt, ALU.add,
                                              accum_out=rk[:, par, 0, t:t + 1]).then_inc(cmp_done, 1)
                        else:
                            seen = (t + 1) * P
                            dve.scalar_tensor_tensor(out=cmp[:, part, 0:seen], in0=srow[:, 0:seen], scalar=own,
                                                     in1=earlier[:, L - seen:L],
                                                     op0=ALU.is_equal, op1=ALU.mult,
                                                     accum_out=rk[:, par, 1, t:t + 1]).then_inc(cmp_done, 1)
                dve.wait_ge(cmp_done, 2 * TT * (f + 1))
                if past(f, 2):
                    dve.wait_ge(rrow_mm, f - 1)
                dve.tensor_tensor(rank[:, par], rk[:, par, 0], rk[:, par, 1], ALU.add).then_inc(rank_done, 1)
            if n is not None:
                normalize(n, 1 - par)
            if f is not None:
                dve.wait_ge(rank_done, f + 1)
                if past(f, 2):
                    dve.wait_ge(sel_mm, 2 * (f - 1))
                for t in range(TT):
                    dve.tensor_scalar(Gm[:, par, t], iota[:], rank[:, par, t:t + 1], None,
                                      ALU.is_equal).then_inc(g_done, 1)
                dve.wait_ge(th_done, f + 1)
                if past(f, 2):
                    dve.wait_ge(rs_done, TT * (f - 1))
                dve.tensor_scalar(wt[:, par], th[:, par], 0.5, 0.5, ALU.mult, ALU.add).then_inc(wt_done, 1)
            if n is not None:
                dve.wait_ge(xn_done, TT * (n + 1))
                if isinstance(n, int) and n == 0:
                    dve.wait_ge(c_in, CONSTANTS)
                for t in range(TT):
                    dve.tensor_tensor_reduce(out=prod[:, t], in0=xn[:, 1 - par, t], in1=router[:], scale=1.0, scalar=0.0,
                                             op0=ALU.mult, op1=ALU.add,
                                             accum_out=score[:, 1 - par, t:t + 1]).then_inc(score_done, 1)
            if b is not None:
                for r in range(RT):
                    dve.wait_ge(y_mm, RT * b + r + 1)
                    if past(b, 1):
                        dve.wait_ge(yl_done, RT * b)
                    dve.tensor_tensor(y[:, r], bank_y[r][:, 0:D], bias2[:], ALU.add).then_inc(y_done, 1)
                    dve.wait_ge(yh_done, RT * b + r + 1)
                    dve.tensor_tensor(yl[:, r], y[:, r], yh[:, r].bitcast(F32), ALU.subtract).then_inc(yl_done, 1)
            if f is not None:
                dve.wait_ge(rrow_mm, f + 1)
                if past(f, 2):
                    dve.wait_ge(scat_mm, TT * (f - 1))
                for r in range(RT):
                    dve.tensor_scalar(GT[:, par, r], bank_row[:], iotac[:, r:r + 1], None,
                                      ALU.is_equal).then_inc(gt_done, 1)
            if b is not None:
                back = 1 - par
                dve.wait_ge(res_done, b + 1)
                dve.wait_ge(wt_done, b + 1)
                if past(b, 1):
                    dve.wait_ge(rs_out, 16 * b)
                for t in range(TT):
                    dve.wait_ge(scat_mm, TT * b + 2 * (t // 2) + 2)
                    dve.scalar_tensor_tensor(out=rs[:, t], in0=bank_back[t // 2][:, (t % 2) * D:(t % 2 + 1) * D],
                                             scalar=wt[:, back, t:t + 1], in1=res[:, back, t],
                                             op0=ALU.mult, op1=ALU.add).then_inc(rs_done, 1)

        def weights(i):
            if i == 0:
                dve.wait_ge(mem_set, 2)
            if i == 1:
                dve.wait_ge(late_in, 4 * 16)
            if i == 2:
                for n, (hi, lo, at, size, scale, _) in enumerate(ATTENTION):
                    dve.wait_ge(attn_hi, n + 1)
                    dve.scalar_tensor_tensor(out=flat(lo), in0=staged(at, size), scalar=scale,
                                             in1=flat(hi).bitcast(F32), op0=ALU.mult,
                                             op1=ALU.subtract).then_inc(attn_lo, 1)

        pipeline(dve, step, weights)
        dve.wait_ge(attn_lo, 3)

    @block.tensor
    def _(pe):
        def step(n, f, b, par):
            back = 1 - par
            if b is not None:
                pe.wait_ge(g_done, TT * (b + 1))
                pe.wait_ge(xl_done, b + 1)
                for part, src in enumerate((xh, xl)):
                    for k in range(DK):
                        for t in range(TT):
                            last = pe.matmul(bank_sel[part][:, k * SEL:(k + 1) * SEL],
                                             src[:, back, t, k * P:(k + 1) * P], Gm[:, back, t],
                                             start=(t == 0), stop=(t == TT - 1))
                    last.then_inc(sel_mm, 1)
            if f is not None:
                pe.wait_ge(score_done, TT * (f + 1))
                if past(f, 1):
                    pe.wait_ge(gt_done, RT * f)
                for t in range(TT):
                    last = pe.transpose(bank_row[:, t * P:(t + 1) * P],
                                        score[:, par, t:t + 1].to_broadcast([P, P]), ident[:])
                last.then_inc(srow_mm, 1)
            if b is not None:
                if isinstance(b, int) and b == 0:
                    pe.wait_ge(w_lo, 2)
                pe.wait_ge(sel_done, 2 * (b + 1))
                if past(b, 1):
                    pe.wait_ge(y_done, RT * b)
                    pe.wait_ge(rs_done, TT * b)
                for c2 in range(FC // 2):
                    if past(b, 1) or c2 >= 2:
                        pe.wait_ge(gelu_done, FC * b + 2 * (c2 - 1))
                    for c in (2 * c2, 2 * c2 + 1):
                        out = bank_h[c2 % 2][:, (c % 2) * SEL:(c % 2 + 1) * SEL]
                        i = 0
                        for w, xs in ((W1h, xsh), (W1l, xsh), (W1h, xsl)):
                            for k in range(DK):
                                last = pe.matmul(out, w[:, k, c * P:(c + 1) * P], xs[:, k * SEL:(k + 1) * SEL],
                                                 start=(i == 0), stop=(i == 3 * DK - 1))
                                i += 1
                    last.then_inc(h_mm, 1)
                for chunks in (range(FC - 4), range(FC - 4, FC - 2), range(FC - 2, FC)):
                    for r in range(RT):
                        for c in chunks:
                            if r == 0 and c % 2 == 0:
                                pe.wait_ge(gh_done, FC // 2 * b + c // 2 + 1)
                            for w in (W2h, W2l):
                                pe.matmul(bank_y[r][:, 0:D], gh[:, c, r * P:(r + 1) * P], w[:, c],
                                          start=(c == 0 and w is W2h), stop=False)
                for r in range(RT):
                    for c in range(FC):
                        if r == 0 and c % 2 == 0:
                            pe.wait_ge(gl_done, FC // 2 * b + c // 2 + 1)
                        last = pe.matmul(bank_y[r][:, 0:D], gl[:, c, r * P:(r + 1) * P], W2h[:, c],
                                         start=False, stop=(c == FC - 1))
                    last.then_inc(y_mm, 1)
            if f is not None:
                pe.wait_ge(rank_done, f + 1)
                pe.wait_ge(srow_done, f + 1)
                for t in range(TT):
                    last = pe.transpose(bank_row[:, t * P:(t + 1) * P],
                                        rank[:, par, t:t + 1].to_broadcast([P, P]), ident[:])
                last.then_inc(rrow_mm, 1)
            if n is not None:
                if isinstance(n, int) and n == 0:
                    pe.wait_ge(c_in, CONSTANTS)
                pe.wait_ge(xn_done, TT * (n + 1))
                if past(n, 1):
                    pe.wait_ge(xtl_done, DK * n)
                for k in range(DK):
                    for t in range(TT):
                        last = pe.transpose(bank_xt[k][:, t * P:(t + 1) * P], xn[:, 1 - par, t, k * P:(k + 1) * P], ident[:])
                    last.then_inc(xt_mm, 1)
            if b is not None:
                pe.wait_ge(yl_done, RT * (b + 1))
                pe.wait_ge(gt_done, RT * (b + 1))
                for t in range(TT):
                    i = 0
                    for r in range(RT):
                        for part in (yh, yl):
                            last = pe.matmul(bank_back[t // 2][:, (t % 2) * D:(t % 2 + 1) * D],
                                             GT[:, back, r, t * P:(t + 1) * P], part[:, r],
                                             start=(i == 0), stop=(i == 2 * RT - 1))
                            i += 1
                    last.then_inc(scat_mm, 1)

        pipeline(pe, step)


def phase_two(nc, dram, ctx, kept):
    def sb(name, shape, dt=F32):
        return ctx.enter_context(nc.sbuf_tensor("a_" + name, shape, dt))

    def ps(name, shape):
        return ctx.enter_context(nc.psum_tensor("a_" + name, shape, F32))

    def sem(name):
        return ctx.enter_context(nc.semaphore("a_" + name))

    PAIRS = H // 2
    OT = PAIRS // 2
    UNITS = TT * G // 2
    Wqh, Wql, Wkh, Wkl, Wvh, Wvl = kept.Wqh, kept.Wql, kept.Wkh, kept.Wkl, kept.Wvh, kept.Wvl
    Woh, Wol = sb("Woh", [P, PAIRS, D], F32R), sb("Wol", [P, PAIRS, D], F32R)
    cos, sin, ident, ones = kept.cos, kept.sin, kept.ident, sb("ones", [P, HD])
    slopes, keyrows = sb("slopes", [P, H]), sb("keyrows", [P, L])
    xT, xt_in, acc = kept.xT, kept.xt_in, kept.acc
    straight, swapped = sb("straight", [P, 2, L]), sb("swapped", [P, 2, L])
    qs, ks = sb("qs", [P, 4, L], F32R), sb("ks", [P, 4, L], F32R)
    q1, q2 = sb("q1", [P, KV, G, L], F32R), sb("q2", [P, 2, G, L], F32R)
    k1, k2 = sb("k1", [P, KV, L], F32R), sb("k2", [P, KV, L], F32R)
    vs, v = sb("vs", [P, TT, KV * HD]), sb("v", [P, KV, TT, HD])
    mx = sb("mx", [P, 2, P])
    nmh, nml = sb("nmh", [P, P], F32R), sb("nml", [P, P], F32R)
    p = sb("p", [P, TT, 2, L])
    psum = sb("psum", [P, 2, L])
    rden, o_raw, o = sb("rden", [P, L]), sb("o_raw", [P, L]), sb("o", [P, L])
    oh, ol = sb("oh", [P, OT, L], F32R), sb("ol", [P, OT, L], F32R)

    bank_m, bank_s = ps("bank_m", [P, 2, L]), ps("bank_s", [P, 2, L])
    bank_o, bank_d = ps("bank_o", [P, L]), ps("bank_d", [P, L])
    bank_f = [ps("bank_f0", [P, L]), ps("bank_f1", [P, L])]
    last_bank = (bank_m[:, 0], bank_m[:, 1], bank_s[:, 0], bank_s[:, 1])
    FIRST = (bank_m, bank_s)

    w_in, w_hi, w_lo, c_in = sem("w_in"), sem("w_hi"), sem("w_lo"), sem("c_in")
    rows_set, mem_set = sem("rows_set"), sem("mem_set")
    acc_in = sem("acc_in")
    rope_mm, v_mm, wo_mm = sem("rope_mm"), sem("v_mm"), sem("wo_mm")
    proj_done, swap_in, kswap_in = sem("proj_done"), sem("swap_in"), sem("kswap_in")
    rot_mul, rot_sum, rope_hi, rope_lo, v_done = (
        sem("rot_mul"), sem("rot_sum"), sem("rope_hi"), sem("rope_lo"), sem("v_done"))
    q1_in = [[sem(f"q1_in{g}_{n}") for n in range(2)] for g in range(KV)]
    k_in, v_in = ([sem(f"{n}{g}") for g in range(KV)] for n in ("k_in", "v_in"))
    q2_in, max_in = [sem(f"q2_in{n}") for n in range(2)], sem("max_in")
    max_mm, max_done, maxT_mm, neg_hi, neg_lo = (
        sem("max_mm"), sem("max_done"), sem("maxT_mm"), sem("neg_hi"), sem("neg_lo"))
    score_mm, exp_done, pv_mm, psum_done, den_mm = (
        sem("score_mm"), sem("exp_done"), sem("pv_mm"), sem("psum_done"), sem("den_mm"))
    raw_done = sem("raw_done")
    ln_done, rden_done, den_read, newton_done = sem("ln_done"), sem("rden_done"), sem("den_read"), sem("newton_done")
    o_done, oh_done, ol_done = sem("o_done"), sem("oh_done"), sem("ol_done")
    acc_done, out_done = sem("acc_done"), sem("out_done")

    SWAP_IN, Q1_IN, Q2_IN, K_IN, V_IN, MAX_IN = 16 * 4, 16 * 2, 16 * 4, 16 * 3, 16, 16 * 2

    def projected_queries(b, g):
        return 4 + 5 * b + (0, 2, 3, 4)[g]

    def projected_keys(b):
        return 4 + 5 * b + 1

    def rotated_queries(b, g):
        return projected_queries(b, g - 1) if g else 5 * b + 3

    def query_rotation(b, g):
        return rotated_queries(b, g - 1) if g else 5 * b + 2

    def key_rotation(b):
        return 0 if isinstance(b, int) and b == 0 else 5 * b

    def is_last(b):
        return isinstance(b, int) and b == B - 1

    def batches(eng, body):
        body(0)
        with eng.Fori(1, B - 1) as b:
            body(b)
        body(B - 1)

    def max_unit(b, g, u):
        ahead = g + (1 if u < UNITS // 2 else 2)
        if is_last(b) and ahead >= KV:
            return None
        return b + ahead // KV, ahead % KV, (u + UNITS // 2) % UNITS

    CONSTANTS = 16 * 2
    stage = p[:].rearrange("p t h l -> p (t h l)")[:, 0:PAIRS * D]

    block = ctx.enter_context(nc.Block())

    @block.sync
    def _(sp):
        def load_acc(b):
            sp.dma_start(acc[:], dram["res"][b].rearrange("(t p) d -> p t d", p=P)).then_inc(acc_in, 16)

        def store_out(b):
            sp.wait_ge(acc_done, 2 * TT * (b + 1))
            sp.dma_start(dram["out"][b].rearrange("(t p) d -> p t d", p=P), acc[:]).then_inc(out_done, 16)

        def swap_halves(dst, src, done):
            for i in range(4):
                j = i ^ 1
                sp.dma_start(dst[i * HALF:(i + 1) * HALF], src[j * HALF:(j + 1) * HALF]).then_inc(done, 16)

        def swap_queries(r, before):
            sp.wait_ge(proj_done, 2 * (r + 1))
            if before is not None:
                sp.wait_ge(rot_sum, 2 * (before + 1))
            swap_halves(swapped[:], straight[:], swap_in)

        def swap_keys(r):
            sp.wait_ge(proj_done, 2 * (r + 1))
            swap_halves(ks[:, 0:2].bitcast(F32), ks[:, 2:4].bitcast(F32), kswap_in)

        def place_q1(f, g, r, n):
            sp.wait_ge(rope_hi, 2 * r + n + 1)
            if past(f, 4):
                sp.wait_ge(score_mm, UNITS * (f - 3))
            for j in range(2):
                sp.dma_start(q1[0:HD, g, 2 * n + j].bitcast(F32),
                             qs[j * HD:(j + 1) * HD, n].bitcast(F32)).then_inc(q1_in[g][n], 16)

        def place_k(f, g, r):
            n, j = g // 2, g % 2
            sp.wait_ge(rope_lo, 2 * r + n + 1)
            if past(f, 4):
                sp.wait_ge(score_mm, UNITS * (f - 3))
            hi, lo = ks[j * HD:(j + 1) * HD, n], ks[j * HD:(j + 1) * HD, 2 + n]
            for dst, src in ((k1[0:HD, g], hi), (k2[HD:P, g], hi), (k2[0:HD, g], lo)):
                sp.dma_start(dst.bitcast(F32), src.bitcast(F32)).then_inc(k_in[g], 16)

        def place_v(f, b, g):
            sp.wait_ge(v_done, 2 * (b + 1))
            if past(f, 4):
                sp.wait_ge(pv_mm, UNITS * (f - 3))
            sp.dma_start(v[:, g], vs[:, :, g * HD:(g + 1) * HD]).then_inc(v_in[g], 16)

        def place_q2(f, slot, r):
            if past(f, 2):
                sp.wait_ge(score_mm, UNITS * (f - 1))
            sp.wait_ge(rope_lo, 2 * (r + 1))
            heads = q2[:, slot].rearrange("p (n j) l -> p n j l", j=2)
            for part in range(2):
                for j in range(2):
                    sp.dma_start(heads[part * HD:(part + 1) * HD, :, j].bitcast(F32),
                                 qs[j * HD:(j + 1) * HD, 2 * part:2 * part + 2].bitcast(F32)).then_inc(q2_in[slot], 16)

        def place_max(f, g):
            for row, src, ready in ((ROW_MAX, nmh, neg_hi), (ROW_MAX + 1, nml, neg_lo)):
                sp.wait_ge(ready, f + 1)
                sp.dma_start(q1[row:row + 1, g].rearrange("o h (t c) -> o (h t) c", c=P).bitcast(F32),
                             src[0:G * TT, :].bitcast(F32)).then_inc(max_in, 16)

        sp.dma_start(slopes[ROW_SLOPE:ROW_MAX, :], dram["slope_rows"]).then_inc(c_in, 16)
        sp.dma_start(keyrows[ROW_SLOPE:ROWS, :], dram["key_rows"]).then_inc(c_in, 16)
        sp.dma_start(stage, dram["Wo"]).then_inc(w_in, 16)
        swap_keys(0)
        swap_queries(1, None)
        place_k(0, 0, 0)
        for n in range(2):
            place_q1(0, 0, 1, n)
        place_q2(0, 0, 1)
        swap_queries(2, 1)
        place_k(1, 1, 0)
        place_v(0, 0, 0)
        place_v(1, 0, 1)
        for n in range(2):
            place_q1(1, 1, 2, n)
        place_max(0, 0)
        swap_queries(3, 2)
        sp.wait_ge(kept.rs_out, 16 * B)
        load_acc(0)

        def body(b):
            for g in range(KV):
                s = 4 * b + g
                ahead = not (is_last(b) and g >= 2)
                if not (is_last(b) and g == KV - 1):
                    place_q2(s + 1, (g + 1) % 2, query_rotation(b, g))
                if g < 2:
                    place_k(s + 2, g + 2, key_rotation(b))
                    place_v(s + 2, b, g + 2)
                elif ahead:
                    place_k(s + 2, g - 2, key_rotation(b + 1))
                if ahead:
                    for n in range(2):
                        place_q1(s + 2, (g + 2) % KV, rotated_queries(b, g), n)
                if g == 1 and past(b, 1):
                    store_out(b - 1)
                if g == 1 and not is_last(b):
                    swap_keys(projected_keys(b))
                if g == 0 and not is_last(b):
                    sp.wait_ge(rope_mm, 2 * (projected_queries(b, 0) + 1))
                    load_xt(sp, dram, kept, b + 1)
                if not (is_last(b) and g == KV - 1):
                    place_max(s + 1, (g + 1) % KV)
                if not (is_last(b) and g >= 1):
                    swap_queries(projected_queries(b, g), rotated_queries(b, g))
                if g == 1 and past(b, 1):
                    sp.wait_ge(out_done, 16 * b)
                    load_acc(b)
                if g == KV - 1 and ahead:
                    place_v(s + 1, b + 1, 0)
                    place_v(s + 2, b + 1, 1)

        batches(sp, body)
        store_out(B - 1)
        sp.wait_ge(out_done, 16 * B)

    @block.gpsimd
    def _(pool):
        pool.memset(mx[:], 0.0).then_inc(mem_set, 1)
        pool.memset(ones[:], 1.0).then_inc(mem_set, 1)

        def lo_queries(r, n):
            pool.wait_ge(rope_hi, 2 * r + n + 1)
            pool.tensor_tensor(qs[:, 2 + n], straight[:, n], qs[:, n].bitcast(F32), ALU.subtract).then_inc(rope_lo, 1)

        def lo_keys(r, n):
            pool.wait_ge(rope_hi, 2 * r + n + 1)
            pool.tensor_tensor(ks[:, 2 + n], ks[:, 2 + n].bitcast(F32), ks[:, n].bitcast(F32),
                               ALU.subtract).then_inc(rope_lo, 1)

        def output_lo(r, slot):
            pool.wait_ge(oh_done, r + 1)
            pool.tensor_tensor(ol[:, slot], o[:], oh[:, slot].bitcast(F32), ALU.subtract).then_inc(ol_done, 1)

        for n in range(2):
            lo_keys(0, n)
        for r in (1, 2):
            for n in range(2):
                lo_queries(r, n)

        def body(b):
            for g in range(KV):
                s = 4 * b + g
                queries = not (is_last(b) and g >= 2)
                for u in range(UNITS):
                    n, kt, r = UNITS * s + u, u % TT, 2 * s + u // TT
                    if kt == 1:
                        pool.wait_ge(exp_done, n + 1)
                        if past(b, 1) or r > 0:
                            pool.wait_ge(den_mm, r)
                        pool.tensor_tensor(psum[:], p[:, 0], p[:, 1], ALU.add).then_inc(psum_done, 1)
                    elif kt > 1:
                        pool.wait_ge(exp_done, n + 1)
                        pool.wait_ge(psum_done, 3 * r + kt - 1)
                        pool.tensor_tensor(psum[:], psum[:], p[:, kt], ALU.add).then_inc(psum_done, 1)
                    if u == 0 and (past(b, 1) or g > 0):
                        output_lo(2 * s - 2, (2 * g - 2) % OT)
                    if u < 2 and g == 2 and not is_last(b):
                        lo_keys(projected_keys(b), u)
                    if u in (2, 3) and queries:
                        lo_queries(rotated_queries(b, g), min(u - 2, 1))
                    if u == 4 and (past(b, 1) or g > 0):
                        output_lo(2 * s - 1, (2 * g - 1) % OT)

        batches(pool, body)
        output_lo(2 * STEPS - 2, OT - 2)
        output_lo(2 * STEPS - 1, OT - 1)

    @block.scalar
    def _(act):
        act.preload_act_table_set("natural_log_exp_and_others")
        def project_queries(r, before):
            for n in range(2):
                act.wait_ge(rope_mm, 2 * r + n + 1)
                if before is not None:
                    act.wait_ge(rope_lo, 2 * before + n + 1)
                act.activation(straight[:, n], bank_f[n][:], ACT.Copy).then_inc(proj_done, 1)

        def project_keys(r, b):
            if b is not None:
                for slot in range(KV):
                    act.wait_ge(k_in[slot], K_IN * (b + 1))
            for n in range(2):
                act.wait_ge(rope_mm, 2 * r + n + 1)
                act.activation(ks[:, 2 + n].bitcast(F32), bank_f[n][:], ACT.Copy).then_inc(proj_done, 1)

        def keys_hi(r, n):
            act.wait_ge(rot_sum, 2 * r + n + 1)
            act.activation(ks[:, n], ks[:, 2 + n].bitcast(F32), ACT.Copy).then_inc(rope_hi, 1)

        def queries_hi(r, b, g, n):
            if past(b, 1) or g > 0:
                placed, last = (b, g - 1) if g else (b - 1, KV - 1)
                act.wait_ge(q1_in[last][n], Q1_IN * (placed + 1))
                act.wait_ge(q2_in[last % 2], Q2_IN * (2 * placed + last // 2 + 1))
            act.wait_ge(rot_sum, 2 * r + n + 1)
            act.activation(qs[:, n], straight[:, n], ACT.Copy).then_inc(rope_hi, 1)

        def values(b):
            for half in range(2):
                act.wait_ge(v_mm, 2 * b + half + 1)
                if past(b, 1):
                    for g in range(KV):
                        act.wait_ge(v_in[g], V_IN * b)
                act.activation(vs[:, 2 * half:2 * half + 2].rearrange("p t d -> p (t d)"), bank_f[half][:],
                               ACT.Copy).then_inc(v_done, 1)

        def output_raw(r):
            act.wait_ge(pv_mm, TT * (r + 1))
            if past(r, 1):
                act.wait_ge(o_done, r)
            act.activation(o_raw[:], bank_o[:], ACT.Copy).then_inc(raw_done, 1)

        def invert(r):
            act.wait_ge(den_mm, r + 1)
            if past(r, 1):
                act.wait_ge(newton_done, r)
            act.activation(rden[:], bank_d[:], ACT.Ln).then_inc(ln_done, 1)
            act.wait_ge(ln_done, r + 1)
            act.activation(rden[:], rden[:], ACT.Exp, scale=-1.0).then_inc(rden_done, 1)

        def output_hi(r, slot, b, g):
            act.wait_ge(o_done, r + 1)
            if g >= 2:
                act.wait_ge(wo_mm, 2 * TT * b + TT)
            elif past(b, 1):
                act.wait_ge(wo_mm, 2 * TT * b)
            act.activation(oh[:, slot], o[:], ACT.Copy).then_inc(oh_done, 1)

        project_keys(0, None)
        project_queries(1, None)
        for n in range(2):
            keys_hi(0, n)
        for n in range(2):
            queries_hi(1, 0, 0, n)
        project_queries(2, 1)
        values(0)
        for n in range(2):
            queries_hi(2, 0, 1, n)
        project_queries(3, 2)
        act.wait_ge(w_in, 16)
        act.activation(flat(Woh), stage, ACT.Copy).then_inc(w_hi, 1)

        def body(b):
            for g in range(KV):
                s = 4 * b + g
                queries = not (is_last(b) and g >= 2)
                for u in range(UNITS):
                    n, kt, r = UNITS * s + u, u % TT, 2 * s + u // TT
                    act.wait_ge(score_mm, n + 1)
                    if past(b, 1) or n >= TT:
                        act.wait_ge(pv_mm, n - TT + 1)
                        act.wait_ge(psum_done, 3 * (r - 1) + max(kt, 1))
                    if isinstance(b, int) and b == 0 and n < 1:
                        act.wait_ge(w_lo, 1)
                    act.activation(p[:, kt], bank_s[:], ACT.Exp).then_inc(exp_done, 1)
                    if u == 0 and (past(b, 1) or g > 0):
                        output_hi(2 * s - 2, (2 * g - 2) % OT, *((b, g - 1) if g else (b - 1, KV - 1)))
                        output_raw(2 * s - 1)
                    if g == 1 and u == 3 and not is_last(b):
                        project_keys(projected_keys(b), b)
                    if g == 1 and u == 7 and not is_last(b):
                        for n in range(2):
                            keys_hi(projected_keys(b), n)
                    if u in (1, 2) and queries:
                        queries_hi(rotated_queries(b, g), b + (g + 2) // KV, (g + 2) % KV, min(u - 1, 1))
                    if u == 2 and (past(b, 1) or g > 0):
                        invert(2 * s - 1)
                    if u == 4 and (past(b, 1) or g > 0):
                        output_hi(2 * s - 1, (2 * g - 1) % OT, *((b, g - 1) if g else (b - 1, KV - 1)))
                    if u == 4 and not (is_last(b) and g >= 1):
                        project_queries(projected_queries(b, g), rotated_queries(b, g))
                    if u == 4:
                        output_raw(2 * s)
                    if u == 3 and g == 2 and not is_last(b):
                        values(b + 1)
                    if u == 6:
                        invert(2 * s)

        batches(act, body)
        output_raw(2 * STEPS - 1)
        output_hi(2 * STEPS - 2, OT - 2, B - 1, KV - 1)
        invert(2 * STEPS - 1)
        output_hi(2 * STEPS - 1, OT - 1, B - 1, KV - 1)

    @block.vector
    def _(dve):
        dve.wait_ge(mem_set, 1)
        dve.wait_ge(c_in, CONSTANTS)
        for g in range(KV):
            dve.tensor_copy(k1[ROW_SLOPE:ROWS, g], keyrows[ROW_SLOPE:ROWS, :]).then_inc(rows_set, 1)
        for g in range(KV):
            dve.tensor_copy(q1[ROW_SLOPE:ROW_MAX, g],
                            slopes[ROW_SLOPE:ROW_MAX, g * G:(g + 1) * G].rearrange("p (h o) -> p h o", o=1)
                            .to_broadcast([ROW_MAX - ROW_SLOPE, G, L])).then_inc(rows_set, 1)

        def rotate(r, n, heads, halves_swapped):
            dve.tensor_tensor(heads, heads, cos[:], ALU.mult).then_inc(rot_mul, 1)
            dve.tensor_tensor(halves_swapped, halves_swapped, sin[:], ALU.mult).then_inc(rot_mul, 1)
            dve.wait_ge(rot_mul, 4 * r + 2 * n + 2)
            dve.tensor_tensor(heads, heads, halves_swapped, ALU.add).then_inc(rot_sum, 1)

        def rotate_queries(r, step, n):
            dve.wait_ge(swap_in, SWAP_IN * (step + 1))
            rotate(r, n, straight[:, n], swapped[:, n])

        def rotate_keys(r, b, n):
            dve.wait_ge(kswap_in, SWAP_IN * (b + 1))
            rotate(r, n, ks[:, 2 + n].bitcast(F32), ks[:, n].bitcast(F32))

        def maxima(b, g, i, bank=bank_m):
            f, parity = 4 * b + g, g % 2
            dve.wait_ge(max_mm, UNITS * f + i + 1)
            if i == 0 and past(f, 2):
                dve.wait_ge(maxT_mm, f - 1)
            dve.tensor_reduce(mx[:, parity, 2 * i:2 * i + 2], bank[:], axis=AX.X, op=ALU.max).then_inc(max_done, 1)

        def negate(f):
            dve.wait_ge(maxT_mm, f + 1)
            if past(f, 1):
                dve.wait_ge(max_in, MAX_IN * f)
            dve.tensor_scalar(nmh[:], bank_d[:, 0:P], -1.0, None, ALU.mult).then_inc(neg_hi, 1)
            dve.wait_ge(neg_hi, f + 1)
            dve.scalar_tensor_tensor(out=nml[:], in0=bank_d[:, 0:P], scalar=-1.0, in1=nmh[:].bitcast(F32),
                                     op0=ALU.mult, op1=ALU.subtract).then_inc(neg_lo, 1)

        def normalize(r):
            dve.wait_ge(rden_done, r + 1)
            if past(r, 1):
                dve.wait_ge(ol_done, r)
            dve.tensor_tensor(o[:], bank_d[:], rden[:], ALU.mult).then_inc(den_read, 1)
            dve.wait_ge(den_read, r + 1)
            dve.scalar_tensor_tensor(out=o[:], in0=o[:], scalar=-2.0, in1=rden[:], op0=ALU.add,
                                     op1=ALU.mult).then_inc(newton_done, 1)
            dve.wait_ge(newton_done, r + 1)
            dve.wait_ge(raw_done, r + 1)
            dve.scalar_tensor_tensor(out=o[:], in0=o[:], scalar=-1.0, in1=o_raw[:], op0=ALU.mult,
                                     op1=ALU.mult).then_inc(o_done, 1)

        def add_output(b, half, t, bank=None):
            bank = bank_f[t % 2] if bank is None else bank
            n = 2 * TT * b + TT * half + t
            dve.wait_ge(wo_mm, n + 1)
            if half == 0:
                dve.wait_ge(acc_in, 16 * (b + 1))
            else:
                dve.wait_ge(acc_done, n - TT + 1)
            dve.tensor_tensor(acc[:, t], bank[:, 0:D], acc[:, t], ALU.add).then_inc(acc_done, 1)

        for n in range(2):
            rotate_keys(0, 0, n)
        for n in range(2):
            rotate_queries(1, 0, n)
        for i in range(UNITS):
            if i == TT:
                for n in range(2):
                    rotate_queries(2, 1, n)
            maxima(0, 0, i, FIRST[i % 2])
        negate(0)
        for i in range(UNITS // 2):
            maxima(0, 1, i, FIRST[i % 2])
        dve.wait_ge(w_hi, 1)
        dve.tensor_tensor(flat(Wol), stage, flat(Woh).bitcast(F32), ALU.subtract).then_inc(w_lo, 1)

        def body(b):
            for g in range(KV):
                s = 4 * b + g
                queries = not (is_last(b) and g >= 2)
                for u in range(UNITS):
                    if (m := max_unit(b, g, u)):
                        maxima(*m)
                    if g == 0 and past(b, 1) and u >= 6:
                        add_output(b - 1, 1, u - 6)
                    if g == 2 and u >= 6:
                        add_output(b, 0, u - 6)
                    if g == 1 and past(b, 1) and u < 2:
                        add_output(b - 1, 1, u + 2)
                    if g == 3 and u < 2:
                        add_output(b, 0, u + 2)
                    if u in (0, 1) and queries:
                        rotate_queries(rotated_queries(b, g), s + 2, min(u, 1))
                    if u == 3 and (past(b, 1) or g > 0):
                        normalize(2 * s - 1)
                    if u == 4 and not (is_last(b) and g == KV - 1):
                        negate(s + 1)
                    if u in (5, 6) and g == 1 and not is_last(b):
                        rotate_keys(projected_keys(b), b + 1, u - 5)
                    if u == 7:
                        normalize(2 * s)

        batches(dve, body)
        normalize(2 * STEPS - 1)
        for t in range(TT):
            add_output(B - 1, 1, t, last_bank[t])

    @block.tensor
    def _(pe):
        def after_projection(bank, r):
            pe.wait_ge(proj_done, 2 * r + bank + 1)

        def after_values(half, b):
            pe.wait_ge(v_done, 2 * b + half + 1)

        def after_output(b, part, t):
            pe.wait_ge(acc_done, 2 * TT * b + TT * part + t + 1)

        def project(wh, wl, head, before):
            for n in range(2):
                before(n)
                columns = slice((head + 2 * n) * HD, (head + 2 * n + 2) * HD)
                i = 0
                for w, part in ((wh, 0), (wl, 0), (wh, 1)):
                    for k in range(DK):
                        last = pe.matmul(bank_f[n][:], w[:, k, columns], xT[:, part, k],
                                         start=(i == 0), stop=(i == 3 * DK - 1))
                        i += 1
                last.then_inc(rope_mm, 1)

        def queries(g, before):
            project(Wqh, Wql, G * g, before)

        def keys(before):
            project(Wkh, Wkl, 0, before)

        def values(half):
            for t in (2 * half, 2 * half + 1):
                i = 0
                for part, w in ((0, Wvh), (1, Wvh), (0, Wvl)):
                    for k in range(DK):
                        last = pe.matmul(bank_f[half][:, (t % 2) * KV * HD:(t % 2 + 1) * KV * HD],
                                         xT[:, part, k, t * P:(t + 1) * P], w[:, k],
                                         start=(i == 0), stop=(i == 3 * DK - 1))
                        i += 1
            last.then_inc(v_mm, 1)

        def output(b, half, t):
            pe.wait_ge(ol_done, PAIRS * b + OT * (half + 1))
            if t >= 2:
                after_output(b, half, t - 2)
            i = 0
            for part, w in ((oh, Woh), (ol, Woh), (oh, Wol)):
                for q in range(OT):
                    last = pe.matmul(bank_f[t % 2][:, 0:D], part[:, q, t * P:(t + 1) * P], w[:, OT * half + q],
                                     start=(i == 0), stop=(i == 3 * OT - 1))
                    i += 1
            last.then_inc(wo_mm, 1)

        def last_output():
            def project(pair, parts, start, stop):
                for t in range(TT):
                    for i, (part, w) in enumerate(parts):
                        last = pe.matmul(last_bank[t][:, 0:D], part[:, pair, t * P:(t + 1) * P], w[:, OT + pair],
                                         start=start and i == 0, stop=stop)
                    if stop:
                        last.then_inc(wo_mm, 1)

            for pair in range(OT - 1):
                pe.wait_ge(ol_done, PAIRS * B - OT + pair + 1)
                project(pair, ((oh, Woh), (ol, Woh), (oh, Wol)), pair == 0, False)
            pe.wait_ge(oh_done, PAIRS * B)
            project(OT - 1, ((oh, Woh), (oh, Wol)), False, False)
            pe.wait_ge(ol_done, PAIRS * B)
            project(OT - 1, ((ol, Woh),), False, True)

        def maxima(b, g, i, bank=bank_m, behind=0):
            f = 4 * b + g
            if i == 0:
                pe.wait_ge(k_in[g], K_IN * (b + 1))
            if i % TT == 0:
                pe.wait_ge(q1_in[g][i // TT], Q1_IN * (b + 1))
            if past(f, 1) or i > behind:
                pe.wait_ge(max_done, UNITS * f + i - behind)
            h = i // 2
            for j in range(2):
                t = 2 * (i % 2) + j
                last = pe.matmul(bank[:, j], q1[0:ROW_MAX, g, h, t * P:(t + 1) * P], k1[0:ROW_MAX, g],
                                 start=True, stop=True)
            last.then_inc(max_mm, 1)

        def transpose_maxima(f, parity):
            pe.wait_ge(max_done, UNITS * (f + 1))
            if past(f, 2):
                pe.wait_ge(den_read, 2 * (f - 1))
            if past(f, 1):
                pe.wait_ge(neg_lo, f)
            pe.transpose(bank_d[:, 0:P], mx[:, parity], ident[:]).then_inc(maxT_mm, 1)

        def scores(b, g, u):
            s, kt = 4 * b + g, u % TT
            if u == 0:
                pe.wait_ge(max_in, MAX_IN * (s + 1))
                pe.wait_ge(q2_in[g % 2], Q2_IN * (2 * b + g // 2 + 1))
            if past(b, 1) or g > 0 or u > 0:
                pe.wait_ge(exp_done, UNITS * s + u)
            else:
                pe.wait_ge(max_done, UNITS + UNITS // 2)
            for j in range(2):
                h = 2 * (u // TT) + j
                pe.matmul(bank_s[:, j], k1[0:ROWS, g, kt * P:(kt + 1) * P], q1[0:ROWS, g, h], start=True, stop=False)
                last = pe.matmul(bank_s[:, j], k2[:, g, kt * P:(kt + 1) * P], q2[:, g % 2, h], start=False, stop=True)
            last.then_inc(score_mm, 1)

        def weighted_values(b, g, u):
            s = 4 * b + g
            kt, r = u % TT, 2 * s + u // TT
            pe.wait_ge(exp_done, UNITS * s + u + 1)
            if u == 0:
                pe.wait_ge(v_in[g], V_IN * (b + 1))
            if kt == 0 and past(r, 1):
                pe.wait_ge(raw_done, r)
            for j in range(2):
                last = pe.matmul(bank_o[j * HD:(j + 1) * HD], v[:, g, kt], p[:, kt, j], start=(kt == 0), stop=(kt == TT - 1))
            last.then_inc(pv_mm, 1)

        def row_sums(r, transposed):
            pe.wait_ge(psum_done, 3 * (r + 1))
            if past(r, 1):
                pe.wait_ge(den_read, r)
            if transposed is not None:
                pe.wait_ge(neg_lo, transposed + 1)
            for j in range(2):
                last = pe.matmul(bank_d[j * HD:(j + 1) * HD], ones[:], psum[:, j], start=True, stop=True)
            last.then_inc(den_mm, 1)

        pe.wait_ge(xt_in, 16)
        pe.wait_ge(mem_set, 2)
        keys(lambda bank: None)
        for g in range(2):
            queries(g, lambda bank: after_projection(bank, g))
        pe.wait_ge(rows_set, 2 * KV)
        for i in range(UNITS):
            if i == TT:
                for half in range(2):
                    after_projection(half, 2)
                    values(half)
            maxima(0, 0, i, FIRST[i % 2], 1)
        transpose_maxima(0, 0)
        queries(2, lambda bank: after_values(bank, 0))
        for i in range(UNITS // 2):
            maxima(0, 1, i, FIRST[i % 2], 1)

        OUTPUTS = {5: (0,), 6: (1,), 7: (2,)}

        def before_keys(b, bank):
            if past(b, 1):
                after_output(b - 1, 1, 2 + bank)
            else:
                after_projection(bank, projected_queries(b, 0))

        def before_queries(b, g, bank):
            if g == 2 and not is_last(b):
                after_values(bank, b + 1)
            elif g == 3:
                after_output(b, 0, 2 + bank)
            else:
                after_projection(bank, projected_queries(b, g) - 1)

        def body(b):
            for g in range(KV):
                s = 4 * b + g
                nxt = not is_last(b)
                for u in range(UNITS):
                    scores(b, g, u)
                    if (m := max_unit(b, g, u)):
                        maxima(*m)
                    if u == 0 and g == 3:
                        output(b, 0, TT - 1)
                    if u == 0 and g == 1 and past(b, 1):
                        output(b - 1, 1, TT - 1)
                    if u == 2 and g == 1 and nxt:
                        pe.wait_ge(xt_in, 16 * (b + 2))
                        keys(lambda bank: before_keys(b, bank))
                    if u == 2 and g == 2 and nxt:
                        for half in range(2):
                            after_projection(half, projected_queries(b, 1))
                            values(half)
                    if u == 4 and (nxt or g == 0):
                        queries((g + 3) % KV, lambda bank: before_queries(b, g, bank))
                    if g == 0 and past(b, 1) and u >= 5:
                        if u < 7:
                            after_projection(u - 5, projected_queries(b, 0))
                        for t in OUTPUTS[u]:
                            output(b - 1, 1, t)
                    if g == 2 and u >= 5:
                        if u < 7:
                            if nxt:
                                after_projection(u - 5, projected_queries(b, 2))
                            else:
                                after_output(b - 1, 1, u - 3)
                        if isinstance(b, int) and b == 0 and u == 5:
                            pe.wait_ge(w_lo, 1)
                        for t in OUTPUTS[u]:
                            output(b, 0, t)
                    if u > 0:
                        weighted_values(b, g, u - 1)
                    elif past(b, 1) or g > 0:
                        weighted_values(b if g else b - 1, (g - 1) % KV, UNITS - 1)
                    if u == 4 and not (is_last(b) and g == KV - 1):
                        transpose_maxima(s + 1, (g + 1) % 2)
                    if u == 1 and (past(b, 1) or g > 0):
                        row_sums(2 * s - 1, None)
                    if u == 5:
                        row_sums(2 * s, None if is_last(b) and g == KV - 1 else s + 1)

        batches(pe, body)
        weighted_values(B - 1, KV - 1, UNITS - 1)
        row_sums(2 * STEPS - 1, None)
        last_output()


def build_program(nc, dram):
    with ExitStack() as both:
        kept = Kept(nc, both)
        with ExitStack() as ctx:
            phase_one(nc, dram, ctx, kept)
        with ExitStack() as ctx:
            phase_two(nc, dram, ctx, kept)


def host_arrays(L0_attn_x, L0_attn_Wq, L0_attn_Wk, L0_attn_Wv, L0_attn_Wo, L0_ffn_w_router,
                L0_ffn_W1, L0_ffn_b1, L0_ffn_W2, L0_ffn_b2):
    def rows(w, k):
        return np.ascontiguousarray(w.reshape((k, P) + w.shape[1:]).swapaxes(0, 1).reshape(P, -1))

    angle = (np.arange(L, dtype=np.float32)[:, None]
             * (np.float32(1.0) / np.float32(10000.0) ** (np.arange(0, HD, 2, dtype=np.float32) / np.float32(HD)))[None])
    slopes = np.array([2.0 ** (-(h + 1) / 2) for h in range(H)], np.float32)
    bits = slopes.view(np.uint32)
    slope_hi = ((bits + 0x800) & 0xFFFFF000).astype(np.uint32).view(np.float32)
    pos = np.arange(L, dtype=np.float32)
    return {
        "x": np.ascontiguousarray(L0_attn_x),
        "Wq": rows(L0_attn_Wq, DK),
        "Wk": rows(L0_attn_Wk, DK),
        "Wv": rows(L0_attn_Wv, DK),
        "Wo": rows(L0_attn_Wo, H * HD // P),
        "W1": rows(L0_ffn_W1, DK),
        "W2": rows(L0_ffn_W2, FC),
        "b1": rows(L0_ffn_b1, FC),
        "b2": np.ascontiguousarray(L0_ffn_b2.reshape(1, D)),
        "router": np.ascontiguousarray(L0_ffn_w_router.reshape(1, D)),
        "cos": np.ascontiguousarray(np.tile(np.cos(angle).T, (4, 1))),
        "sin": np.ascontiguousarray(np.tile(np.concatenate([-np.sin(angle).T, np.sin(angle).T]), (2, 1))),
        "ident": np.eye(P, dtype=np.float32),
        "iota": np.arange(SEL, dtype=np.float32).reshape(1, SEL),
        "iotac": np.ascontiguousarray(np.arange(SEL, dtype=np.float32).reshape(RT, P).T),
        "earlier": np.ascontiguousarray(np.arange(P)[None, :] < np.arange(P)[:, None]).astype(np.float32),
        "slope_rows": np.stack([slope_hi, slopes - slope_hi]),
        "key_rows": np.stack([pos, pos, np.ones_like(pos), np.ones_like(pos)]),
    }


def kernel(**inputs):
    import concourse.bacc as bacc
    from concourse.bass_utils import run_bass_kernel_spmd

    nc = bacc.Bacc("TRN2", target_bir_lowering=False, num_devices=1)
    arrays = host_arrays(**{name: np.asarray(a) for name, a in inputs.items()})
    dram = {name: nc.dram_tensor("in_" + name, a.shape, mybir.dt.from_np(a.dtype), kind="ExternalInput").ap()
            for name, a in arrays.items()}
    dram["xt"] = nc.dram_tensor("scratch_xt", [B, 2, P, DK, L], F32R).ap()
    dram["res"] = nc.dram_tensor("scratch_res", [B, L, D], F32).ap()
    dram["out"] = nc.dram_tensor("out", [B, L, D], F32, kind="ExternalOutput").ap()
    build_program(nc, dram)
    result = run_bass_kernel_spmd(nc, [{"in_" + name: a for name, a in arrays.items()}], core_ids=[0])
    return result.results[0]["out"]
```
